# Optimizing a Trainium2 kernel written in Bass

```python
import numpy as np
import jax
import jax.numpy as jnp

def _softmax(x, axis=-1):
    return jax.nn.softmax(x, axis=axis)

def _gelu(x):
    return jax.nn.gelu(x, approximate=True)

def _silu(x):
    return jax.nn.silu(x)

def _sigmoid(x):
    return jax.nn.sigmoid(x)

def _layernorm(x, axis=-1, eps=1e-05):
    m = jnp.mean(x, axis=axis, keepdims=True)
    v = jnp.var(x, axis=axis, keepdims=True)
    return (x - m) / jnp.sqrt(v + eps)

def _scatter_add(tgt, idx, src, axis=0):
    return tgt.at[idx].add(src)

def _segment_sum(src, seg, n):
    return jax.ops.segment_sum(src, seg, n)
kernel_name = 'mk_cond_seq_d2_seqx_r4_8fc394'

def setup_inputs(seed: int=0):
    np.random.seed(seed)
    _w = jnp.asarray

    def _rec_inputs():
        import jax
        import jax.numpy as jnp
        _rk = jax.random.key(seed)
        x = -0.0002928 + 1 * jax.random.normal(jax.random.fold_in(_rk, 1), (64, 64, 256), jnp.float32)
        _lenS = 64 - jax.random.randint(jax.random.fold_in(_rk, 7), (64,), 0, max(1, 64 // 4) + 1, jnp.int32)
        _lenS2 = 64 - jax.random.randint(jax.random.fold_in(_rk, 8), (64,), 0, max(1, 64 // 4) + 1, jnp.int32)
        cond_1024 = 0.000887014 + 1.03683 * jax.random.normal(jax.random.fold_in(_rk, 11), (64, 256), jnp.float32)
        _validS = jnp.arange(64)[None, :] < _lenS[:, None]
        _validS2 = jnp.arange(64)[None, :] < _lenS2[:, None]
        _causal = jnp.tril(jnp.ones((64, 64), dtype=bool))
        mask_BxS_bf0 = jnp.logical_not(jnp.ones((64, 64), dtype=bool))
        return (x, cond_1024, mask_BxS_bf0)
    x, cond_1024, mask_BxS_bf0 = _rec_inputs()

    def _L0_cond_setup():
        import math
        import jax, jax.numpy as jnp
        import numpy as np
        H = 256
        NH = 16
        HD = H // NH
        CD = 256
        MLP = 1024
        EPS = 1e-05

        def _layernorm(x):
            mu = jnp.mean(x, axis=-1, keepdims=True)
            var = jnp.var(x, axis=-1, keepdims=True)
            return (x - mu) * jax.lax.rsqrt(var + EPS)

        def _adaln(x, cond, W, b):
            ss = cond @ W.T + b
            scale, shift = jnp.split(ss, 2, axis=-1)
            return _layernorm(x) * (1.0 + scale[:, None, :]) + shift[:, None, :]
        key = jax.random.key(seed)
        ks = jax.random.split(key, 16)
        s = 0.02
        inp = {'x': jax.random.normal(ks[0], (2, 512, H), jnp.float32), 'cond': jax.random.normal(ks[1], (2, CD), jnp.float32), 'key_padding_mask': jnp.zeros((2, 512), dtype=bool), 'w_adaln1': jax.random.normal(ks[2], (2 * H, CD), jnp.float32) * s, 'b_adaln1': jnp.zeros((2 * H,), jnp.float32), 'w_adaln2': jax.random.normal(ks[3], (2 * H, CD), jnp.float32) * s, 'b_adaln2': jnp.zeros((2 * H,), jnp.float32), 'wq': jax.random.normal(ks[4], (H, H), jnp.float32) * s, 'bq': jnp.zeros((H,), jnp.float32), 'wk': jax.random.normal(ks[5], (H, H), jnp.float32) * s, 'bk': jnp.zeros((H,), jnp.float32), 'wv': jax.random.normal(ks[6], (H, H), jnp.float32) * s, 'bv': jnp.zeros((H,), jnp.float32), 'wo': jax.random.normal(ks[7], (H, H), jnp.float32) * s, 'bo': jnp.zeros((H,), jnp.float32), 'w1': jax.random.normal(ks[8], (MLP, H), jnp.float32) * s, 'b1': jnp.zeros((MLP,), jnp.float32), 'w2': jax.random.normal(ks[9], (H, MLP), jnp.float32) * s, 'b2': jnp.zeros((H,), jnp.float32)}
        return inp
    _L0_cond_all = _L0_cond_setup()
    _L0_cond_in = {k: v for k, v in _L0_cond_all.items() if k in ('w_adaln1', 'b_adaln1', 'w_adaln2', 'b_adaln2', 'wq', 'bq', 'wk', 'bk', 'wv', 'bv', 'wo', 'bo', 'w1', 'b1', 'w2', 'b2')}
    del _L0_cond_all

    def _L1_cond_setup():
        import jax, jax.numpy as jnp
        import numpy as np
        H = 256
        NH = 16
        DH = H // NH
        MLP = 4 * H
        EPS = 1e-05

        def _ln(x):
            m = jnp.mean(x, axis=-1, keepdims=True)
            v = jnp.mean((x - m) ** 2, axis=-1, keepdims=True)
            return (x - m) * jax.lax.rsqrt(v + EPS)

        def _modulate(x, shift, scale):
            return x * (1.0 + scale[:, None, :]) + shift[:, None, :]
        key = jax.random.key(seed)
        ks = jax.random.split(key, 12)
        s = 1.0 / np.sqrt(H)
        inp = {'x': jax.random.normal(ks[0], (8, 256, H), jnp.float32), 'c': jax.random.normal(ks[1], (8, H), jnp.float32), 'Wc': jax.random.normal(ks[2], (H, 6 * H), jnp.float32) * s, 'bc': jnp.zeros((6 * H,), jnp.float32), 'Wq': jax.random.normal(ks[3], (H, H), jnp.float32) * s, 'bq': jnp.zeros((H,), jnp.float32), 'Wk': jax.random.normal(ks[4], (H, H), jnp.float32) * s, 'bk': jnp.zeros((H,), jnp.float32), 'Wv': jax.random.normal(ks[5], (H, H), jnp.float32) * s, 'bv': jnp.zeros((H,), jnp.float32), 'Wo': jax.random.normal(ks[6], (H, H), jnp.float32) * s, 'bo': jnp.zeros((H,), jnp.float32), 'W1': jax.random.normal(ks[7], (H, MLP), jnp.float32) * s, 'b1': jnp.zeros((MLP,), jnp.float32), 'W2': jax.random.normal(ks[8], (MLP, H), jnp.float32) * (1.0 / np.sqrt(MLP)), 'b2': jnp.zeros((H,), jnp.float32)}
        return inp
    _L1_cond_all = _L1_cond_setup()
    _L1_cond_in = {k: v for k, v in _L1_cond_all.items() if k in ('Wc', 'bc', 'Wq', 'bq', 'Wk', 'bk', 'Wv', 'bv', 'Wo', 'bo', 'W1', 'b1', 'W2', 'b2')}
    del _L1_cond_all
    return {'x': x, 'cond_1024': cond_1024, 'mask_BxS_bf0': mask_BxS_bf0, 'L0_cond_w_adaln1': _L0_cond_in['w_adaln1'], 'L0_cond_b_adaln1': _L0_cond_in['b_adaln1'], 'L0_cond_w_adaln2': _L0_cond_in['w_adaln2'], 'L0_cond_b_adaln2': _L0_cond_in['b_adaln2'], 'L0_cond_wq': _L0_cond_in['wq'], 'L0_cond_bq': _L0_cond_in['bq'], 'L0_cond_wk': _L0_cond_in['wk'], 'L0_cond_bk': _L0_cond_in['bk'], 'L0_cond_wv': _L0_cond_in['wv'], 'L0_cond_bv': _L0_cond_in['bv'], 'L0_cond_wo': _L0_cond_in['wo'], 'L0_cond_bo': _L0_cond_in['bo'], 'L0_cond_w1': _L0_cond_in['w1'], 'L0_cond_b1': _L0_cond_in['b1'], 'L0_cond_w2': _L0_cond_in['w2'], 'L0_cond_b2': _L0_cond_in['b2'], 'L1_cond_Wc': _L1_cond_in['Wc'], 'L1_cond_bc': _L1_cond_in['bc'], 'L1_cond_Wq': _L1_cond_in['Wq'], 'L1_cond_bq': _L1_cond_in['bq'], 'L1_cond_Wk': _L1_cond_in['Wk'], 'L1_cond_bk': _L1_cond_in['bk'], 'L1_cond_Wv': _L1_cond_in['Wv'], 'L1_cond_bv': _L1_cond_in['bv'], 'L1_cond_Wo': _L1_cond_in['Wo'], 'L1_cond_bo': _L1_cond_in['bo'], 'L1_cond_W1': _L1_cond_in['W1'], 'L1_cond_b1': _L1_cond_in['b1'], 'L1_cond_W2': _L1_cond_in['W2'], 'L1_cond_b2': _L1_cond_in['b2']}

def reference(x, cond_1024, mask_BxS_bf0, L0_cond_w_adaln1, L0_cond_b_adaln1, L0_cond_w_adaln2, L0_cond_b_adaln2, L0_cond_wq, L0_cond_bq, L0_cond_wk, L0_cond_bk, L0_cond_wv, L0_cond_bv, L0_cond_wo, L0_cond_bo, L0_cond_w1, L0_cond_b1, L0_cond_w2, L0_cond_b2, L1_cond_Wc, L1_cond_bc, L1_cond_Wq, L1_cond_bq, L1_cond_Wk, L1_cond_bk, L1_cond_Wv, L1_cond_bv, L1_cond_Wo, L1_cond_bo, L1_cond_W1, L1_cond_b1, L1_cond_W2, L1_cond_b2):
    import jax
    import jax.numpy as jnp

    def _L0_cond_ref(x, cond, key_padding_mask, w_adaln1, b_adaln1, w_adaln2, b_adaln2, wq, bq, wk, bk, wv, bv, wo, bo, w1, b1, w2, b2):
        import math
        import jax, jax.numpy as jnp
        import numpy as np
        H = 256
        NH = 16
        HD = H // NH
        CD = 256
        MLP = 1024
        EPS = 1e-05

        def _layernorm(x):
            mu = jnp.mean(x, axis=-1, keepdims=True)
            var = jnp.var(x, axis=-1, keepdims=True)
            return (x - mu) * jax.lax.rsqrt(var + EPS)

        def _adaln(x, cond, W, b):
            ss = cond @ W.T + b
            scale, shift = jnp.split(ss, 2, axis=-1)
            return _layernorm(x) * (1.0 + scale[:, None, :]) + shift[:, None, :]
        B, L, D = x.shape
        normed = _adaln(x, cond, w_adaln1, b_adaln1)
        q = (normed @ wq.T + bq).reshape(B, L, NH, HD)
        k = (normed @ wk.T + bk).reshape(B, L, NH, HD)
        v = (normed @ wv.T + bv).reshape(B, L, NH, HD)
        scale = math.sqrt(HD)
        scores = jnp.einsum('blhd,bmhd->bhlm', q, k) / scale
        scores = jnp.where(key_padding_mask[:, None, None, :], -jnp.inf, scores)
        attn = jax.nn.softmax(scores, axis=-1)
        attn_out = jnp.einsum('bhlm,bmhd->blhd', attn, v).reshape(B, L, D)
        x = x + attn_out @ wo.T + bo
        normed = _adaln(x, cond, w_adaln2, b_adaln2)
        h = jax.nn.gelu(normed @ w1.T + b1, approximate=False)
        x = x + h @ w2.T + b2
        return x

    def _L1_cond_ref(x, c, Wc, bc, Wq, bq, Wk, bk, Wv, bv, Wo, bo, W1, b1, W2, b2):
        import jax, jax.numpy as jnp
        import numpy as np
        H = 256
        NH = 16
        DH = H // NH
        MLP = 4 * H
        EPS = 1e-05

        def _ln(x):
            m = jnp.mean(x, axis=-1, keepdims=True)
            v = jnp.mean((x - m) ** 2, axis=-1, keepdims=True)
            return (x - m) * jax.lax.rsqrt(v + EPS)

        def _modulate(x, shift, scale):
            return x * (1.0 + scale[:, None, :]) + shift[:, None, :]
        B, S, _ = x.shape
        c6 = jax.nn.silu(c) @ Wc + bc
        sh_msa, sc_msa, g_msa, sh_mlp, sc_mlp, g_mlp = jnp.split(c6, 6, axis=-1)
        xm = _modulate(_ln(x), sh_msa, sc_msa)
        q = (xm @ Wq + bq).reshape(B, S, NH, DH)
        k = (xm @ Wk + bk).reshape(B, S, NH, DH)
        v = (xm @ Wv + bv).reshape(B, S, NH, DH)
        q = q / DH
        w = jnp.einsum('bqhc,bkhc->bhqk', q, k)
        w = jax.nn.softmax(w, axis=-1)
        y = jnp.einsum('bhqk,bkhc->bqhc', w, v).reshape(B, S, H)
        x = x + g_msa[:, None, :] * (y @ Wo + bo)
        xm2 = _modulate(_ln(x), sh_mlp, sc_mlp)
        h = jax.nn.gelu(xm2 @ W1 + b1, approximate=False)
        x = x + g_mlp[:, None, :] * (h @ W2 + b2)
        return x
    x = _L0_cond_ref(x, cond_1024, mask_BxS_bf0, L0_cond_w_adaln1, L0_cond_b_adaln1, L0_cond_w_adaln2, L0_cond_b_adaln2, L0_cond_wq, L0_cond_bq, L0_cond_wk, L0_cond_bk, L0_cond_wv, L0_cond_bv, L0_cond_wo, L0_cond_bo, L0_cond_w1, L0_cond_b1, L0_cond_w2, L0_cond_b2)
    x = _L1_cond_ref(x, cond_1024, L1_cond_Wc, L1_cond_bc, L1_cond_Wq, L1_cond_bq, L1_cond_Wk, L1_cond_bk, L1_cond_Wv, L1_cond_bv, L1_cond_Wo, L1_cond_bo, L1_cond_W1, L1_cond_b1, L1_cond_W2, L1_cond_b2)
    return x

_drawn_inputs = setup_inputs


def setup_inputs(seed=0):
    import zlib

    import numpy as np

    out = dict(_drawn_inputs(seed))
    spreads = {'L0_cond_b_adaln1': (0.0, 0.771),
     'L0_cond_b_adaln2': (0.0, 0.504),
     'L0_cond_bq': (0.0, 0.8),
     'L0_cond_bk': (0.0, 2.0),
     'L0_cond_bv': (0.0, 0.1),
     'L0_cond_bo': (0.0, 0.1),
     'L0_cond_b1': (0.0, 0.1),
     'L0_cond_b2': (0.0, 0.1),
     'L1_cond_bc': (0.0, 0.1),
     'L1_cond_bq': (0.0, 2.0),
     'L1_cond_bk': (0.0, 2.0),
     'L1_cond_bv': (0.0, 0.1),
     'L1_cond_bo': (0.0, 0.1),
     'L1_cond_b1': (0.0, 0.1),
     'L1_cond_b2': (0.0, 0.1)}
    factors = {'L0_cond_wq': 8.0, 'L0_cond_wk': 8.0}
    for name, (base, spread) in spreads.items():
        noise = np.random.default_rng([zlib.crc32(name.encode()), seed]).standard_normal(out[name].shape)
        drawn = base * np.exp(spread * noise) if base else spread * noise
        out[name] = jnp.asarray(drawn.astype(out[name].dtype))
    for name, factor in factors.items():
        out[name] = (out[name] * factor).astype(out[name].dtype)
    return out
```

```python
from contextlib import ExitStack

import numpy as np
import concourse.bass as bass
from concourse import mybir
from concourse.alu_op_type import AluOpType as ALU

ACT = mybir.ActivationFunctionType
AX = mybir.AxisListType
F32 = mybir.dt.float32
F32R = mybir.dt.float32r
U8 = mybir.dt.uint8

P = 128
B, S, H = 64, 64, 256
NH = 16
HD = H // NH
MLP = 1024
EPS = 1e-5
GB = 4
G = GB * S
T = G // P
C = H // P
NG = B // GB
HC = MLP // P
HP = HC // 2
ROUNDS = NG // 2 - 1
HT = 4
RT = 2
PAIR = 2 * (HD + 1)
NPAIR = NH // 2
SCORE_SCALE = (HD ** -0.5, 1.0 / HD)
BIG = 3e38

PIECES = ["ada1", "qk0", "vo0", "ada2", "w10a", "w10b", "w20a", "w20b",
          "c0", "c1", "c2", "qk1", "vo1", "w11a", "w11b", "w21a", "w21b"]
ADAPTIVE = ["ada1", "ada2", "c0", "c1", "c2"]
SPLIT = [n for n in PIECES if n not in ADAPTIVE]
PIECE = 1024
RING = 3
EARLY = 4
COLS, NCOLS = {}, 0
for _name, _n in (("bq0", C), ("bk0", C), ("bq1", C), ("bk1", C), ("b10", HC), ("b11", HC),
                  ("ada1", 4), ("ada2", 4), ("c0", 4), ("c1", 4), ("c2", 4), ("head", HT)):
    COLS[_name] = (NCOLS, _n)
    NCOLS += _n
ROWS = ["bv0", "bo0", "b20", "bv1", "bo1", "b21", "bg0", "bg1"]


class Unit:

    def __init__(self, r, c):
        self.static = isinstance(r, int)
        self.index = 4 * r + c
        self.layer = c % 4 // 2
        self.stream = c % 2
        self.turn = r + c // 4
        self.group = 2 * r + 2 * (c // 4) + c % 2


def build(nc, x, cond_t, mask, pieces, cols, rows, ident_in, out):
    ctx = ExitStack()
    with ctx:
        def sb(name, shape, dt=F32):
            return ctx.enter_context(nc.sbuf_tensor(name, shape, dt))

        def bank(name):
            return ctx.enter_context(nc.psum_tensor(name, [P, 512], F32))

        x_g = x.rearrange("b s f -> (b s) f").rearrange("(g t p) f -> g p t f", t=T, p=P)
        out_g = out.rearrange("b s f -> (b s) f").rearrange("(g t p) f -> g p t f", t=T, p=P)
        gates_dram = nc.dram_tensor("gates_dram", [2, B, H], F32, kind="Internal").ap()
        gates_g = gates_dram.rearrange("w (g t h) f -> g w h t f", t=T, h=2)

        wqk = [[sb(f"wqk{l}{h}", [P, C, 2 * H], F32R) for h in ("hi", "lo")] for l in range(2)]
        wvo = [[sb(f"wvo{l}{h}", [P, C, 2 * H], F32R) for h in ("hi", "lo")] for l in range(2)]
        w1 = [[sb(f"w1{l}{h}", [P, 2, C, MLP // 2], F32R) for h in ("hi", "lo")] for l in range(2)]
        w2 = [[sb(f"w2{l}{h}", [P, HC, H], F32R) for h in ("hi", "lo")] for l in range(2)]
        ring = sb("ring", [P, RING, PIECE])
        ident = sb("ident", [P, P])
        col = sb("col", [P, NCOLS])
        row = sb("row", [P, len(ROWS), H])
        mask8 = sb("mask8", [P, NG * T, S], U8)
        cond = sb("cond", [P, C, B])
        silu_cond = sb("silu_cond", [P, C, B])
        minus_half = sb("minus_half", [P, T])
        scale = [[sb(f"scale{l}{w}", [P, C, B]) for w in range(2)] for l in range(2)]
        shift = [[sb(f"shift{l}{w}", [P, C, B]) for w in range(2)] for l in range(2)]
        xin = [sb(f"xin{s}", [P, T, H]) for s in "AB"]
        xres = [sb(f"xres{s}", [P, T, H]) for s in "AB"]
        xout = sb("xout", [P, T, H])
        gate_rows = xout[0:B, :, :]
        part = [sb(f"part{w}", [P, T, H]) for w in range(2)]
        gate = [sb(f"gate{w}", [P, T, H]) for w in range(2)]
        stats = [sb(f"stats{w}", [P, T, 6]) for w in range(2)]
        moments = [sb(f"moments{w}", [P, T, 2]) for w in range(2)]
        var_eps = [sb(f"var_eps{w}", [P, T]) for w in range(2)]
        rstd = [sb(f"rstd{w}", [P, T]) for w in range(2)]
        xn = [sb(f"xn{w}", [P, T, H]) for w in range(2)]
        mod = [sb(f"mod{w}", [P, C, G]) for w in range(2)]
        nrm = [[sb(f"nrm{w}{h}", [P, C, G], F32R) for h in ("hi", "lo")] for w in range(2)]
        maskf = sb("maskf", [P, T, S])
        qt = sb("qt", [P, C, G])
        kt = sb("kt", [P, C, G])
        kheads = sb("kheads", [P, C, HT, G])
        vt = sb("vt", [P, T, H])
        vswap = sb("vswap", [P, T, H])
        vpairs = sb("vpairs", [P, GB, NPAIR, PAIR])
        prob = sb("prob", [P, T, RT, C * HT, S])
        top = sb("top", [P, T, RT, C * HT])
        probt = sb("probt", [P, T, RT, 4, P])
        inv = sb("inv", [P, T, NH])
        yn = sb("yn", [P, T, H])
        yt = [sb(f"yt{h}", [P, C, G], F32R) for h in ("hi", "lo")]
        hid = sb("hid", [P, 2, 2, G])
        ht = [sb(f"ht{h}", [P, HC, G], F32R) for h in ("hi", "lo")]

        b_turn = bank("b_turn")
        b_mix = [bank("b_mix0"), bank("b_mix1")]
        b_score = [[bank(f"b_score{t}{r}") for r in range(RT)] for t in range(T)]
        b_y = [b_score[t][0] for t in range(T)]
        b_wo = b_score[0][1]
        b_yt = b_score[1][1]
        b_pt = [b_mix, [b_score[1][1], b_score[0][1]]]
        b_mlp = bank("b_mlp")

        names = """const_in xin_A xin_B gate_in0 gate_in1 gate_out out_stored piece_in0 piece_in1 piece_in2
            w_hi w_lo ada_mm ada_read pool_ready dve_ready silu
            stat0 aggr0 var0 rstd0 xn0 turned0 scaled0 mod0 hi0 lo0
            stat1 aggr1 var1 rstd1 xn1 turned1 scaled1 mod1 hi1 lo1
            q_mm k_mm v_mm q_done k_done kheads_done v_done v_swapped vpairs_done score_mm mask_ready masked topped shifted exp_done
            pt_mm pt_act pt_dve pv_mm inv_done y_done y_turned y_hi y_lo wo_mm
            w1_mm h_f32 h_hi h_lo w2_mm
            base0 sum0 gated0 res0 base1 sum1 gated1 res1""".split()
        s = {n: ctx.enter_context(nc.semaphore(f"s_{n}")) for n in names}

        def await_unit(eng, name, u, back=0, per=1, k=1):
            if not u.static or u.index >= back:
                eng.wait_ge(s[name], per * (u.index - back) + k)

        def await_group(eng, name, u, back=0, per=1, k=1):
            if not u.static or u.group >= back:
                eng.wait_ge(s[name], per * (u.group - back) + k)

        def await_alone(eng, name, u, back=0, per=1, k=1):
            if not u.static or u.index >= back:
                eng.wait_ge(s[name], per * (u.index - back) + k)
                eng.nop(nofuse=True)

        def await_x(eng, u):
            eng.wait_ge(s["xin_" + "AB"[u.stream]], 16 * u.turn + 16)

        def await_residual(eng, w, u):
            if u.layer == 0:
                await_unit(eng, f"sum{w}", u)
            else:
                await_group(eng, f"res{w}", u)

        def c_(name, j):
            return col[:, COLS[name][0] + j:COLS[name][0] + j + 1]

        def row_all(name):
            return row[:, ROWS.index(name), :].unsqueeze(1).broadcast_to([P, T, H])

        def tokens(m, u):
            return m[:, :, bass.ds(u.group * GB, GB)].unsqueeze(3).broadcast_to([P, C, GB, S])

        def by_seq(ap):
            return ap.rearrange("p c (b s) -> p c b s", b=GB)

        def by_chunk(bk):
            return bk[:, :].rearrange("p (c n) -> p c n", c=2)

        def raw(ap):
            return ap.bitcast(F32)

        def split_parts(name):
            kind, l = name[:2], int(name[2])
            if kind == "qk":
                return [w[:, :, :].rearrange("p c n -> p (c n)") for w in wqk[l]]
            if kind == "vo":
                return [w[:, :, :].rearrange("p c n -> p (c n)") for w in wvo[l]]
            part_no = "ab".index(name[3])
            if kind == "w1":
                return [w[:, part_no].rearrange("p c n -> p (c n)") for w in w1[l]]
            half = HC // 2
            return [w[:, part_no * half:(part_no + 1) * half].rearrange("p c n -> p (c n)") for w in w2[l]]

        def await_piece(eng, name):
            n = PIECES.index(name)
            eng.wait_ge(s[f"piece_in{n % RING}"], 16 * (n // RING) + 16)

        def staged(name):
            return ring[:, PIECES.index(name) % RING, :]

        def run_slots(eng, slot):
            slot(Unit(0, 0), None, Unit(0, 1))
            for q in range(1, 5):
                slot(Unit(0, q), Unit(0, q - 1), Unit(0, q + 1))
            with eng.Fori(1, ROUNDS) as i:
                for q in range(1, 5):
                    slot(Unit(i, q), Unit(i, q - 1), Unit(i, q + 1))
            for q in range(1, 4):
                slot(Unit(ROUNDS, q), Unit(ROUNDS, q - 1), Unit(ROUNDS, q + 1) if q < 3 else None)
            slot(None, Unit(ROUNDS, 3), None)

        block = ctx.enter_context(nc.Block())

        @block.sync
        def _(sp):
            def load_x(u):
                if not u.static or u.turn >= 1:
                    sp.wait_ge(s["xn0"], T * (u.index - 4) + T)
                    sp.wait_ge(s["base0"], u.group - 2 + 1)
                sp.dma_start(xin[u.stream][:, :, :], x_g[u.group]).then_inc(s["xin_" + "AB"[u.stream]], 16)

            def load_gate(w, u):
                await_group(sp, f"gated{w}", u, back=1)
                for half in range(2):
                    sp.dma_start(gate[w][64 * half:64 * half + 64, :, :],
                                 gates_g[u.group, w, half].partition_broadcast(64)).then_inc(s[f"gate_in{w}"], 16)

            def load_piece(n):
                if n >= RING:
                    old = PIECES[n - RING]
                    if old in ADAPTIVE:
                        sp.wait_ge(s["ada_mm"], ADAPTIVE.index(old) + 1)
                    else:
                        sp.wait_ge(s["w_hi"], SPLIT.index(old) + 1)
                        sp.wait_ge(s["w_lo"], SPLIT.index(old) + 1)
                sp.dma_start(ring[:, n % RING, :], pieces[n]).then_inc(s[f"piece_in{n % RING}"], 16)

            load_x(Unit(0, 0))
            sp.dma_start(ident[:, :], ident_in).then_inc(s["const_in"], 16)
            sp.dma_start(cond[:, :, :], cond_t.rearrange("(c p) b -> p c b", p=P)).then_inc(s["const_in"], 16)
            sp.dma_start(col[:, :], cols).then_inc(s["const_in"], 16)
            load_piece(0)
            load_piece(1)
            sp.dma_start(row[:, :, :], rows.partition_broadcast(P)).then_inc(s["const_in"], 16)
            for half in range(2):
                sp.dma_start(mask8[64 * half:64 * half + 64, :, :],
                             mask.rearrange("(t h) k -> h t k", h=2)[half].partition_broadcast(64))\
                  .then_inc(s["const_in"], 16)
            load_x(Unit(0, 1))
            for n in range(2, len(PIECES)):
                load_piece(n)
            sp.wait_ge(s["ada_read"], ADA_READS)
            sp.dma_start(gates_dram.rearrange("w b f -> b w f"), gate_rows[:, :, :]).then_inc(s["gate_out"], 16)
            sp.wait_ge(s["gate_out"], 16)

            def swap_values(u):
                await_unit(sp, "v_done", u)
                await_unit(sp, "vpairs_done", u, back=1, per=4, k=4)
                for half in range(2):
                    sp.dma_start(vswap[64 * half:64 * half + 64, :, :], vt[64 - 64 * half:128 - 64 * half, :, :])\
                      .then_inc(s["v_swapped"], 16)

            def slot(a, m, nx):
                if a is not None:
                    swap_values(a)
                if m is not None and m.layer == 1:
                    load_gate(1, m)
                if a is not None and a.layer == 1:
                    load_gate(0, a)
                if m is not None and m.layer == 1:
                    await_group(sp, "res1", m)
                    sp.dma_start(out_g[m.group], xout[:, :, :]).then_inc(s["out_stored"], 16)

            def round_(i):
                for q in range(1, 5):
                    if q in (2, 3):
                        load_x(Unit(i, q + 2))
                    slot(Unit(i, q), Unit(i, q - 1), Unit(i, q + 1))

            slot(Unit(0, 0), None, Unit(0, 1))
            round_(0)
            with sp.Fori(1, ROUNDS) as i:
                round_(i)
            for q in range(1, 4):
                slot(Unit(ROUNDS, q), Unit(ROUNDS, q - 1), None)
            slot(None, Unit(ROUNDS, 3), None)
            sp.wait_ge(s["out_stored"], 16 * NG)

        @block.tensor
        def _(pe):
            def product(o, n_k, lhs, rhs, moving=False, lo_wait=None):
                for k in range(n_k):
                    for weight in range(2):
                        pair = (weight, 0) if moving else (0, weight)
                        pe.matmul(o, lhs(k, pair[0]), rhs(k, pair[1]), start=(k == 0 and weight == 0), stop=False)
                if lo_wait is not None:
                    lo_wait()
                for k in range(n_k):
                    mm = pe.matmul(o, lhs(k, 0 if moving else 1), rhs(k, 1 if moving else 0), start=False,
                                   stop=(k == n_k - 1))
                return mm

            def turn(src, bk):
                for t in range(T):
                    for c in range(C):
                        mm = pe.transpose(bk[:, c * G + t * P:c * G + (t + 1) * P],
                                          src[:, t, c * P:(c + 1) * P], ident[:, :])
                return mm

            def turn_norm0(u):
                await_unit(pe, "xn0", u, per=T, k=T)
                turn(xn[0], b_turn).then_inc(s["turned0"], 1)

            def adaptive(name):
                n = ADAPTIVE.index(name)
                await_piece(pe, name)
                if n:
                    pe.wait_ge(s["ada_read"], sum(READS[:n]))
                cc = cond if name in ("ada1", "ada2") else silu_cond
                w = staged(name).rearrange("p (c n) -> p c n", c=C)
                if cc is silu_cond:
                    pe.wait_ge(s["silu"], 1)
                for j in FEATURE_CHUNKS[name]:
                    for k in range(C):
                        mm = pe.matmul(b_mlp[:, j * B:(j + 1) * B], w[:, k, j * P:(j + 1) * P], cc[:, k, :],
                                       start=(k == 0), stop=(k == C - 1))
                if name in GATE_COLUMNS:
                    a = GATE_COLUMNS[name]
                    for k in range(C):
                        mm = pe.matmul(b_mlp[0:B, 256:512], cc[:, k, :], w[:, k, a:a + H],
                                       start=(k == 0), stop=(k == C - 1))
                mm.then_inc(s["ada_mm"], 1)

            def project(u):
                w, x_ = wqk[u.layer], nrm[0]
                await_unit(pe, "hi0", u)
                for which, name, free in ((1, "k_mm", "pt_dve"), (0, "q_mm", "pt_act")):
                    await_unit(pe, free, u, back=1, per=T, k=1)
                    for c in range(C):
                        a = which * H + c * P
                        mm = product(b_mix[which][:, c * G:(c + 1) * G], C, lambda k, h: w[h][:, k, a:a + P],
                                     lambda k, h: x_[h][:, k, :], moving=True,
                                     lo_wait=lambda: which == 1 and c == 0 and await_unit(pe, "lo0", u))
                    mm.then_inc(s[name], 1)
                if u.static and u.index == 0:
                    pe.wait_ge(s["w_lo"], SPLIT.index("vo0") + 1)
                await_unit(pe, "q_done", u, per=C, k=C)
                for t in range(T):
                    mm = product(b_mix[0][:, t * H:(t + 1) * H], C, lambda k, h: x_[h][:, k, t * P:(t + 1) * P],
                                 lambda k, h: wvo[u.layer][h][:, k, 0:H])
                mm.then_inc(s["v_mm"], 1)

            def scores(u, t):
                for r in range(RT):
                    if t == 0 and r == 0:
                        await_alone(pe, "kheads_done", u, per=HT, k=HT)
                    if r == 0:
                        await_alone(pe, "y_done", u, back=1, per=T, k=t + 1)
                    else:
                        await_alone(pe, ("sum0", "y_lo")[t], u, back=1)
                    rows_ = slice(64 * r, 64 * r + 64)
                    for c in range(C):
                        for j in range(2):
                            b = slice((2 * t + j) * S, (2 * t + j + 1) * S)
                            mm = pe.matmul(b_score[t][r][64 * j:64 * j + 64, c * HT * S:(c + 1) * HT * S],
                                           qt[rows_, c, b], kheads[rows_, c, :, b], start=True, stop=True)
                    mm.then_inc(s["score_mm"], 1)

            def turn_norm1(u):
                await_unit(pe, "xn1", u, per=T, k=T)
                turn(xn[1], b_turn).then_inc(s["turned1"], 1)

            def hidden(u, a):
                w = w1[u.layer]
                await_unit(pe, "hi1", u)
                for jp in range(HP):
                    if jp >= 2:
                        await_unit(pe, "h_hi", u, per=HC, k=2 * (jp - 1))
                    elif a is not None:
                        await_unit(pe, ("v_done", "k_done")[jp], a, per=(1, C)[jp], k=(1, C)[jp])
                    else:
                        await_unit(pe, ("pt_act", "pt_dve")[jp], u, per=T, k=1)
                    for e in range(2):
                        j = 2 * jp + e
                        hc = slice(j % 4 * P, j % 4 * P + P)
                        mm = product(b_mix[jp % 2][:, e * G:(e + 1) * G],
                                     C, lambda k, h: w[h][:, j // 4, k, hc], lambda k, h: nrm[1][h][:, k, :],
                                     moving=True, lo_wait=lambda: j == 0 and await_unit(pe, "lo1", u))
                    mm.then_inc(s["w1_mm"], 1)

            def mlp_out(u):
                await_unit(pe, "sum1", u, back=1)
                def hidden_hi(k, h):
                    if t == 0 and h == 0 and k % 2 == 0:
                        await_unit(pe, "h_hi", u, per=HC, k=k + 2)
                    return ht[h][:, k, t * P:(t + 1) * P]

                for t in range(T):
                    mm = product(b_mlp[:, t * H:(t + 1) * H], HC, hidden_hi, lambda k, h: w2[u.layer][h][:, k, :],
                                 lo_wait=lambda: t == 0 and await_unit(pe, "h_lo", u, per=HP, k=HP))
                mm.then_inc(s["w2_mm"], 1)

            def turn_probs(u, m, t):
                for r in range(RT):
                    await_unit(pe, "exp_done", u, per=4, k=r + 1 if t == 0 else 4)
                    if t == 0 and m is not None:
                        await_unit(pe, "h_hi", m, per=HC, k=2 * (2 + r + 1))
                    elif t == 0:
                        await_unit(pe, ("v_done", "k_done")[r], u, per=(1, C)[r], k=(1, C)[r])
                    for q in range(4):
                        mm = pe.transpose(b_pt[t][r][:, q * P:(q + 1) * P],
                                          prob[:, t, r, 2 * q:2 * q + 2, :].rearrange("p h k -> p (h k)"), ident[:, :])
                    mm.then_inc(s["pt_mm"], 1)

            def values(u, t):
                for r in range(RT):
                    if t == 0 and r == 0:
                        await_alone(pe, "vpairs_done", u, per=4, k=4)
                    await_alone(pe, ("pt_act", "pt_dve")[r], u, per=T, k=t + 1)
                    for q in range(4):
                        pair = 4 * (q // 2) + 2 * r + q % 2
                        for j in range(2):
                            mm = pe.matmul(b_y[t][64 * j:64 * j + 64, pair * PAIR:(pair + 1) * PAIR],
                                           probt[:, t, r, q, 64 * j:64 * j + 64], vpairs[:, 2 * t + j, pair, :],
                                           start=True, stop=True)
                mm.then_inc(s["pv_mm"], 1)

            def turn_y(u):
                await_unit(pe, "y_done", u, per=T, k=T)
                turn(yn, b_yt).then_inc(s["y_turned"], 1)

            def attention_out(u):
                await_unit(pe, "y_hi", u)
                for t in range(T):
                    mm = product(b_wo[:, t * H:(t + 1) * H], C, lambda k, h: yt[h][:, k, t * P:(t + 1) * P],
                                 lambda k, h: wvo[u.layer][h][:, k, H:2 * H],
                                 lo_wait=lambda: t == 0 and await_unit(pe, "y_lo", u))
                mm.then_inc(s["wo_mm"], 1)

            pe.wait_ge(s["const_in"], 16 * CONSTS)
            turn_norm0(Unit(0, 0))
            adaptive("ada1")

            def slot(a, m, nx):
                first = m is None
                if a is not None:
                    if first:
                        pe.wait_ge(s["w_lo"], SPLIT.index("qk0") + 1)
                    project(a)
                if m is not None:
                    turn_norm1(m)
                if a is not None:
                    scores(a, 0)
                    scores(a, 1)
                if m is not None:
                    hidden(m, a)
                    mlp_out(m)
                if first:
                    for name in ADAPTIVE[1:]:
                        adaptive(name)
                if a is not None:
                    turn_probs(a, m, 0)
                    turn_probs(a, m, 1)
                    values(a, 0)
                    values(a, 1)
                    turn_y(a)
                    if nx is not None:
                        if m is None:
                            await_unit(pe, "scaled0", a)
                        else:
                            await_unit(pe, "scaled1", m)
                        turn_norm0(nx)
                    attention_out(a)
                if first:
                    pe.wait_ge(s["w_lo"], len(SPLIT))

            run_slots(pe, slot)

        @block.scalar
        def _(act):
            def split_hi(name):
                await_piece(act, name)
                act.activation(split_parts(name)[0], staged(name), ACT.Copy).then_inc(s["w_hi"], 1)

            def norm_hi(w, u):
                await_unit(act, f"mod{w}", u)
                if w == 1:
                    await_unit(act, "w1_mm", u, back=1, per=HP, k=HP)
                else:
                    await_unit(act, "v_mm", u, back=1)
                act.activation(nrm[w][0][:, :, :], mod[w][:, :, :], ACT.Copy).then_inc(s[f"hi{w}"], 1)

            act.wait_ge(s["const_in"], 16 * CONSTS)
            act.activation(silu_cond[:, :, :], cond[:, :, :], ACT.Silu).then_inc(s["silu"], 1)
            for name in PIECES[:EARLY]:
                if name in SPLIT:
                    split_hi(name)
            norm_hi(0, Unit(0, 0))

            def slot(a, m, nx):
                if a is not None:
                    for name, dst in (("k", kt), ("q", qt)):
                        await_unit(act, f"{name}_mm", a)
                        if name == "q":
                            await_unit(act, "score_mm", a, back=1, per=4, k=4)
                        else:
                            await_unit(act, "kheads_done", a, back=1, per=HT, k=HT)
                        for c in range(C):
                            act.activation(dst[:, c, :], b_mix["qk".index(name)][:, c * G:(c + 1) * G], ACT.Identity,
                                           bias=c_(f"b{name}{a.layer}", c)).then_inc(s[f"{name}_done"], 1)
                if m is not None:
                    norm_hi(1, m)
                    await_unit(act, "w2_mm", m, back=1)
                    for jp in range(HP):
                        await_unit(act, "w1_mm", m, per=HP, k=jp + 1)
                        if jp >= 2:
                            await_unit(act, "h_lo", m, per=HP, k=jp - 1)
                        else:
                            await_unit(act, "h_lo", m, back=1, per=HP, k=HP)
                        for e in range(2):
                            j = 2 * jp + e
                            src, bias = b_mix[jp % 2][:, e * G:(e + 1) * G], c_(f"b1{m.layer}", j)
                            act.activation(hid[:, jp % 2, e, :], src, ACT.Gelu, bias=bias).then_inc(s["h_f32"], 1)
                            act.activation(ht[0][:, j, :], src, ACT.Gelu, bias=bias).then_inc(s["h_hi"], 1)
                else:
                    for name in PIECES[EARLY:]:
                        if name in SPLIT:
                            split_hi(name)
                if a is not None:
                    for t in range(T):
                        for r in range(RT):
                            await_unit(act, "shifted", a, per=4, k=2 * t + r + 1)
                            act.activation(prob[:, t, r], prob[:, t, r], ACT.Exp, scale=SCORE_SCALE[a.layer])\
                               .then_inc(s["exp_done"], 1)
                    for t in range(T):
                        await_unit(act, "pt_mm", a, per=4, k=2 * t + 1)
                        await_unit(act, "pv_mm", a, back=1, per=T, k=T)
                        act.activation(probt[:, t, 0], b_pt[t][0][:, :].rearrange("p (q n) -> p q n", q=4), ACT.Copy)\
                           .then_inc(s["pt_act"], 1)
                    await_unit(act, "y_turned", a)
                    await_unit(act, "wo_mm", a, back=1)
                    act.activation(yt[0][:, :, :], by_chunk(b_yt), ACT.Copy).then_inc(s["y_hi"], 1)
                    if nx is not None:
                        norm_hi(0, nx)

            run_slots(act, slot)

        @block.vector
        def _(dve):
            def split_lo(name):
                dve.wait_ge(s["w_hi"], SPLIT.index(name) + 1)
                hi, lo = split_parts(name)
                dve.tensor_tensor(lo, staged(name), raw(hi), ALU.subtract).then_inc(s["w_lo"], 1)

            def adaptive(name):
                n = ADAPTIVE.index(name)
                dve.wait_ge(s["ada_mm"], n + 1)
                for j, (dst, chunk, plus) in FEATURE_TARGETS(name, scale, shift).items():
                    dve.tensor_scalar(dst[:, chunk, :], b_mlp[:, j * B:(j + 1) * B], c_(name, j), plus,
                                      ALU.add, ALU.add).then_inc(s["ada_read"], 1)
                if name in GATE_COLUMNS:
                    w = 0 if name == "c1" else 1
                    dve.tensor_tensor(gate_rows[:, w, :], b_mlp[0:B, 256:512], row[0:B, ROWS.index(f"bg{w}"), :],
                                      ALU.add).then_inc(s["ada_read"], 1)

            def moments_of(w, u, src):
                for t in range(T):
                    dve.bn_stats(stats[w][:, t, :], src[:, t, :]).then_inc(s[f"stat{w}"], 1)
                await_alone(dve, f"stat{w}", u, per=T, k=T)
                for t in range(T):
                    dve.bn_aggr(moments[w][:, t, :], stats[w][:, t, :]).then_inc(s[f"aggr{w}"], 1)
                await_unit(dve, f"aggr{w}", u, per=T, k=T)
                dve.tensor_scalar(var_eps[w][:, :], moments[w][:, :, 1], EPS, None, ALU.add).then_inc(s[f"var{w}"], 1)

            def normed(w, u, src):
                await_unit(dve, f"rstd{w}", u)
                await_unit(dve, f"turned{w}", u, back=1)
                for t in range(T):
                    dve.tensor_scalar(xn[w][:, t, :], src[:, t, :], moments[w][:, t, 0:1], rstd[w][:, t:t + 1],
                                      ALU.subtract, ALU.mult).then_inc(s[f"xn{w}"], 1)

            def source(u):
                return xin[u.stream] if u.layer == 0 else xres[u.stream]

            def times_scale(w, u):
                await_unit(dve, f"turned{w}", u)
                await_unit(dve, f"lo{w}", u, back=1)
                dve.tensor_tensor(by_seq(mod[w][:, :, :]), by_seq(by_chunk(b_turn)), tokens(scale[u.layer][w], u),
                                  ALU.mult).then_inc(s[f"scaled{w}"], 1)

            def norm_lo(w, u):
                await_unit(dve, f"hi{w}", u)
                dve.tensor_tensor(nrm[w][1][:, :, :], mod[w][:, :, :], raw(nrm[w][0][:, :, :]), ALU.subtract)\
                   .then_inc(s[f"lo{w}"], 1)

            def take_product(w, u, bk, bias):
                await_unit(dve, ("wo_mm", "w2_mm")[w], u)
                if u.layer == 0:
                    await_group(dve, f"base{w}", u)
                    dve.tensor_tensor(xres[u.stream][:, :, :], by_chunk(bk), part[w][:, :, :], ALU.add)\
                       .then_inc(s[f"sum{w}"], 1)
                    return
                dve.tensor_tensor(part[w][:, :, :], by_chunk(bk), row_all(bias), ALU.add).then_inc(s[f"sum{w}"], 1)

            def add_gated(w, u):
                if u.layer == 0:
                    return
                await_group(dve, f"gated{w}", u)
                if w == 1 and not (u.static and u.group == 0):
                    dve.wait_ge(s["out_stored"], 16 * u.group)
                dst = xres[u.stream] if w == 0 else xout
                dve.tensor_tensor(dst[:, :, :], xres[u.stream][:, :, :], part[w][:, :, :], ALU.add)\
                   .then_inc(s[f"res{w}"], 1)

            def pair_values(u, swapped):
                if swapped:
                    await_unit(dve, "v_swapped", u, per=32, k=32)
                else:
                    await_unit(dve, "v_done", u)
                    await_unit(dve, "pv_mm", u, back=1, per=T, k=T)
                for odd in range(2):
                    half = slice(64 * odd, 64 * odd + 64)
                    src = (vt, vswap)[swapped][half, :, :].rearrange("p t (n o d) -> p t n o d", n=NPAIR, o=2)
                    dve.tensor_copy(vpairs[half, odd ^ swapped:GB:2, :, odd * (HD + 1):odd * (HD + 1) + HD],
                                    src[:, :, :, odd, :]).then_inc(s["vpairs_done"], 1)

            def softmax(u, t):
                for r in range(RT):
                    k = 2 * t + r + 1
                    src = b_score[t][r][:, :].rearrange("p (h k) -> p h k", h=C * HT)
                    dst = prob[:, t, r]
                    await_unit(dve, "score_mm", u, per=4, k=k)
                    await_unit(dve, "pt_mm", u, back=1, per=4, k=4)
                    if u.layer == 0:
                        dve.tensor_tensor(dst, src, maskf[:, t, :].unsqueeze(1).broadcast_to([P, C * HT, S]),
                                          ALU.add).then_inc(s["masked"], 1)
                        await_group(dve, "masked", u, per=4, k=k)
                        src = dst
                    dve.tensor_reduce(top[:, t, r, :], src, AX.X, ALU.max).then_inc(s["topped"], 1)
                    await_unit(dve, "topped", u, per=4, k=k)
                    dve.tensor_tensor(dst, src, top[:, t, r, :].unsqueeze(2).broadcast_to([P, C * HT, S]),
                                      ALU.subtract).then_inc(s["shifted"], 1)

            dve.memset(vpairs[:, :, :, :], 0.0).then_inc(s["dve_ready"], 1)
            dve.wait_ge(s["dve_ready"], 1)
            dve.memset(vpairs[0:64, :, :, HD:HD + 1], 1.0).then_inc(s["dve_ready"], 1)
            dve.memset(vpairs[64:128, :, :, PAIR - 1:PAIR], 1.0).then_inc(s["dve_ready"], 1)
            dve.wait_ge(s["dve_ready"], 3)
            dve.wait_ge(s["const_in"], 16 * CONSTS)
            await_x(dve, Unit(0, 0))
            moments_of(0, Unit(0, 0), xin[0])
            normed(0, Unit(0, 0), xin[0])
            adaptive("ada1")
            dve.wait_ge(s["ada_read"], READS[0])
            times_scale(0, Unit(0, 0))
            split_lo("qk0")
            split_lo("vo0")
            norm_lo(0, Unit(0, 0))

            def slot(a, m, nx):
                if a is not None:
                    await_unit(dve, "k_done", a, per=C, k=C)
                    await_unit(dve, "score_mm", a, back=1, per=4, k=4)
                    for j in range(HT):
                        dve.tensor_scalar(kheads[:, :, j, :], kt[:, :, :], c_("head", j), None, ALU.mult)\
                           .then_inc(s["kheads_done"], 1)
                    await_unit(dve, "v_mm", a)
                    await_unit(dve, "vpairs_done", a, back=1, per=4, k=4)
                    dve.tensor_tensor(vt[:, :, :], by_chunk(b_mix[0]), row_all(f"bv{a.layer}"), ALU.add)\
                       .then_inc(s["v_done"], 1)
                    pair_values(a, 0)
                if m is not None:
                    times_scale(1, m)
                if a is not None:
                    if a.layer == 0:
                        await_group(dve, "masked", a, back=1, per=4, k=4)
                        dve.tensor_scalar(maskf[:, :, :], mask8[:, bass.ds(a.group * T, T), :], -BIG, BIG,
                                          ALU.mult, ALU.mult).then_inc(s["mask_ready"], 1)
                        await_group(dve, "mask_ready", a)
                    softmax(a, 0)
                if m is not None:
                    norm_lo(1, m)
                if a is not None:
                    softmax(a, 1)
                if m is not None:
                    take_product(1, m, b_mlp, f"b2{m.layer}")
                else:
                    for name in PIECES[3:]:
                        if name in SPLIT:
                            split_lo(name)
                        else:
                            adaptive(name)
                    dve.wait_ge(s["ada_read"], ADA_READS)
                if a is not None:
                    pair_values(a, 1)
                    for t in range(T):
                        await_unit(dve, "pt_mm", a, per=4, k=2 * t + 2)
                        await_unit(dve, "pv_mm", a, back=1, per=T, k=T)
                        dve.tensor_copy(probt[:, t, 1], b_pt[t][1][:, :].rearrange("p (q n) -> p q n", q=4))\
                           .then_inc(s["pt_dve"], 1)
                if m is not None:
                    add_gated(1, m)
                if nx is not None:
                    if nx.layer == 0:
                        await_x(dve, nx)
                    else:
                        await_residual(dve, 1, m)
                    moments_of(0, nx, source(nx))
                if a is not None:
                    for t in range(T):
                        sums = b_y[t][:, 0:NPAIR * PAIR].rearrange("p (h n) -> p h n", h=NH)
                        await_unit(dve, "pv_mm", a, per=T, k=t + 1)
                        dve.reciprocal(inv[:, t, :], sums[:, :, HD]).then_inc(s["inv_done"], 1)
                        await_unit(dve, "inv_done", a, per=T, k=t + 1)
                        await_unit(dve, "y_turned", a, back=1)
                        dve.tensor_tensor(yn[:, t, :].rearrange("p (h d) -> p h d", h=NH), sums[:, :, 0:HD],
                                          inv[:, t, :].unsqueeze(2).broadcast_to([P, NH, HD]), ALU.mult)\
                           .then_inc(s["y_done"], 1)
                        if t == 0 and nx is not None:
                            normed(0, nx, source(nx))
                    if nx is not None:
                        times_scale(0, nx)
                    await_unit(dve, "y_hi", a)
                    dve.tensor_tensor(yt[1][:, :, :], by_chunk(b_yt), raw(yt[0][:, :, :]), ALU.subtract)\
                       .then_inc(s["y_lo"], 1)
                    if nx is not None:
                        norm_lo(0, nx)
                    take_product(0, a, b_wo, f"bo{a.layer}")
                    add_gated(0, a)
                    await_residual(dve, 0, a)
                    moments_of(1, a, xres[a.stream])
                    normed(1, a, xres[a.stream])

            run_slots(dve, slot)

        @block.gpsimd
        def _(pool):
            def inverse_root(w, u):
                await_unit(pool, f"var{w}", u)
                pool.tensor_tensor(rstd[w][:, :], var_eps[w][:, :], minus_half[:, :], ALU.pow).then_inc(s[f"rstd{w}"], 1)

            def plus_shift(w, u):
                await_unit(pool, f"scaled{w}", u)
                pool.tensor_tensor(by_seq(mod[w][:, :, :]), by_seq(mod[w][:, :, :]), tokens(shift[u.layer][w], u),
                                   ALU.add).then_inc(s[f"mod{w}"], 1)

            def base(w, u, src, bias):
                pool.tensor_tensor(part[w][:, :, :], src[:, :, :], row_all(bias), ALU.add).then_inc(s[f"base{w}"], 1)

            def gated(w, u):
                await_unit(pool, f"sum{w}", u)
                pool.wait_ge(s[f"gate_in{w}"], 32 * u.group + 32)
                pool.tensor_tensor(part[w][:, :, :], part[w][:, :, :], gate[w][:, :, :], ALU.mult)\
                    .then_inc(s[f"gated{w}"], 1)

            pool.memset(minus_half[:, :], -0.5).then_inc(s["pool_ready"], 1)
            pool.wait_ge(s["pool_ready"], 1)
            inverse_root(0, Unit(0, 0))
            pool.wait_ge(s["const_in"], 16 * CONSTS)
            pool.wait_ge(s["ada_read"], READS[0])
            plus_shift(0, Unit(0, 0))

            def slot(a, m, nx):
                if a is not None and a.layer == 0:
                    await_x(pool, a)
                    if m is not None:
                        await_residual(pool, 0, m)
                    base(0, a, xin[a.stream], "bo0")
                if m is not None:
                    if m.layer == 0:
                        await_unit(pool, "sum0", m)
                        if m.stream == 1:
                            await_unit(pool, "sum1", m, back=1)
                        elif not m.static or m.group > 0:
                            pool.wait_ge(s["res1"], m.group)
                        base(1, m, xres[m.stream], "b20")
                    plus_shift(1, m)
                    for jp in range(HP):
                        await_unit(pool, "h_hi", m, per=HC, k=2 * jp + 2)
                        if jp == 0:
                            await_unit(pool, "w2_mm", m, back=1)
                        pool.tensor_tensor(ht[1][:, 2 * jp:2 * jp + 2, :], hid[:, jp % 2], raw(ht[0][:, 2 * jp:2 * jp + 2, :]),
                                           ALU.subtract).then_inc(s["h_lo"], 1)
                    if m.layer == 1:
                        gated(1, m)
                if nx is not None:
                    inverse_root(0, nx)
                    if m is None:
                        pool.wait_ge(s["ada_read"], ADA_READS)
                    plus_shift(0, nx)
                if a is not None:
                    if a.layer == 1:
                        gated(0, a)
                    inverse_root(1, a)

            run_slots(pool, slot)


FEATURE_CHUNKS = {"ada1": range(4), "ada2": range(4), "c0": range(4), "c1": (2, 3), "c2": (0, 1)}
GATE_COLUMNS = {"c1": 0, "c2": H}
READS = [len(FEATURE_CHUNKS[n]) + (n in GATE_COLUMNS) for n in ADAPTIVE]
ADA_READS = sum(READS)
CONSTS = 6


def FEATURE_TARGETS(name, scale, shift):
    one, none = (scale, 1.0), (shift, 0.0)
    parts = {"ada1": {0: (one, 0, 0), 2: (none, 0, 0)}, "ada2": {0: (one, 0, 1), 2: (none, 0, 1)},
             "c0": {0: (none, 1, 0), 2: (one, 1, 0)}, "c1": {2: (none, 1, 1)}, "c2": {0: (one, 1, 1)}}[name]
    return {j + c: (kind[0][l][w], c, kind[1]) for j, (kind, l, w) in parts.items() for c in range(C)}


def kernel(x, cond_1024, mask_BxS_bf0, **w):
    import concourse.bacc as bacc
    from concourse.bass_utils import run_bass_kernel_spmd as run

    w = {k: np.asarray(v) for k, v in w.items()}

    def wide(m):
        return m.reshape(C, P, 2 * H).transpose(1, 0, 2).reshape(P, PIECE)

    def tall(m):
        return m.reshape(HC // 2, P, H).transpose(1, 0, 2).reshape(P, PIECE)

    L0 = {n: w[f"L0_cond_{n}"].T for n in ("w_adaln1", "w_adaln2", "wq", "wk", "wv", "wo", "w1", "w2")}
    L1 = {n.lower(): w[f"L1_cond_{n}"] for n in ("Wc", "Wq", "Wk", "Wv", "Wo", "W1", "W2")}
    pieces = {"ada1": wide(L0["w_adaln1"]), "ada2": wide(L0["w_adaln2"])}
    for j in range(3):
        pieces[f"c{j}"] = wide(L1["wc"][:, j * 512:(j + 1) * 512])
    for l, m in enumerate((L0, L1)):
        pieces[f"qk{l}"] = wide(np.concatenate([m["wq"], m["wk"]], 1))
        pieces[f"vo{l}"] = wide(np.concatenate([m["wv"], m["wo"]], 1))
        for j, h in enumerate("ab"):
            pieces[f"w1{l}{h}"] = wide(m["w1"][:, j * 512:(j + 1) * 512])
            pieces[f"w2{l}{h}"] = tall(m["w2"][j * 512:(j + 1) * 512])
    pieces = np.stack([pieces[n] for n in PIECES])

    def by_column(v):
        return v.reshape(-1, P).T

    bc = w["L1_cond_bc"]
    head = (np.arange(P)[:, None] % 64 // HD == np.arange(HT)[None, :]).astype(np.float32)
    cols = {"bq0": w["L0_cond_bq"], "bk0": w["L0_cond_bk"], "bq1": w["L1_cond_bq"], "bk1": w["L1_cond_bk"],
            "b10": w["L0_cond_b1"], "b11": w["L1_cond_b1"], "ada1": w["L0_cond_b_adaln1"],
            "ada2": w["L0_cond_b_adaln2"], "c0": bc[0:512], "c1": bc[512:1024], "c2": bc[1024:1536]}
    cols = np.concatenate([by_column(cols[n]) if n != "head" else head for n in COLS], 1)
    rows = {"bv0": w["L0_cond_bv"], "bo0": w["L0_cond_bo"], "b20": w["L0_cond_b2"], "bv1": w["L1_cond_bv"],
            "bo1": w["L1_cond_bo"], "b21": w["L1_cond_b2"], "bg0": bc[512:768], "bg1": bc[1280:1536]}
    rows = np.stack([rows[n] for n in ROWS])
    arrays = {"x": np.asarray(x), "cond_t": np.asarray(cond_1024).T, "mask": np.asarray(mask_BxS_bf0),
              "pieces": pieces, "cols": cols, "rows": rows, "ident": np.eye(P, dtype=np.float32)}
    arrays = {f"in_{k}": np.ascontiguousarray(v) for k, v in arrays.items()}

    nc = bacc.Bacc("TRN2", target_bir_lowering=False, num_devices=1, dynamic_dma_scratch_size=1024)
    aps = [nc.dram_tensor(k, v.shape, mybir.dt.from_np(v.dtype), kind="ExternalInput").ap() for k, v in arrays.items()]
    out = nc.dram_tensor("out", (B, S, H), F32, kind="ExternalOutput").ap()
    build(nc, *aps, out)
    return run(nc, [arrays], core_ids=[0]).results[0]["out"]
```

```python
from contextlib import ExitStack

import numpy as np
import concourse.bass as bass
from concourse import mybir
from concourse.alu_op_type import AluOpType as ALU

ACT = mybir.ActivationFunctionType
AX = mybir.AxisListType
F32 = mybir.dt.float32
F32R = mybir.dt.float32r
U8 = mybir.dt.uint8

P = 128
B, S, H = 64, 64, 256
NH = 16
HD = H // NH
MLP = 1024
EPS = 1e-5
GB = 4
G = GB * S
T = G // P
C = H // P
NG = B // GB
HC = MLP // P
HP = HC // 2
ROUNDS = NG // 2 - 1
HT = 4
RT = 2
PAIR = 2 * (HD + 1)
NPAIR = NH // 2
SCORE_SCALE = (HD ** -0.5, 1.0 / HD)
BIG = 3e38

PIECES = ["ada1", "qk0", "vo0", "ada2", "w10a", "w10b", "w20a", "w20b",
          "c0", "c1", "c2", "qk1", "vo1", "w11a", "w11b", "w21a", "w21b"]
ADAPTIVE = ["ada1", "ada2", "c0", "c1", "c2"]
SPLIT = [n for n in PIECES if n not in ADAPTIVE]
PIECE = 1024
RING = 3
EARLY = 4
COLS, NCOLS = {}, 0
for _name, _n in (("bq0", C), ("bk0", C), ("bq1", C), ("bk1", C), ("b10", HC), ("b11", HC),
                  ("ada1", 4), ("ada2", 4), ("c0", 4), ("c1", 4), ("c2", 4), ("head", HT)):
    COLS[_name] = (NCOLS, _n)
    NCOLS += _n
ROWS = ["bv0", "bo0", "b20", "bv1", "bo1", "b21", "bg0", "bg1"]


class Unit:

    def __init__(self, r, c):
        self.r, self.c = r, c
        self.static = isinstance(r, int)
        self.index = 4 * r + c
        self.layer = c % 4 // 2
        self.stream = c % 2
        self.turn = r + c // 4
        self.group = 2 * r + 2 * (c // 4) + c % 2


def build(nc, x, cond_t, mask, pieces, cols, rows, ident_in, out):
    ctx = ExitStack()
    with ctx:
        def sb(name, shape, dt=F32):
            return ctx.enter_context(nc.sbuf_tensor(name, shape, dt))

        def bank(name):
            return ctx.enter_context(nc.psum_tensor(name, [P, 512], F32))

        x_g = x.rearrange("b s f -> (b s) f").rearrange("(g t p) f -> g p t f", t=T, p=P)
        out_g = out.rearrange("b s f -> (b s) f").rearrange("(g t p) f -> g p t f", t=T, p=P)
        gates_dram = nc.dram_tensor("gates_dram", [2, B, H], F32, kind="Internal").ap()
        gates_g = gates_dram.rearrange("w (g t h) f -> g w h t f", t=T, h=2)

        wqk = [[sb(f"wqk{l}{h}", [P, C, 2 * H], F32R) for h in ("hi", "lo")] for l in range(2)]
        wvo = [[sb(f"wvo{l}{h}", [P, C, 2 * H], F32R) for h in ("hi", "lo")] for l in range(2)]
        w1 = [[sb(f"w1{l}{h}", [P, 2, C, MLP // 2], F32R) for h in ("hi", "lo")] for l in range(2)]
        w2 = [[sb(f"w2{l}{h}", [P, HC, H], F32R) for h in ("hi", "lo")] for l in range(2)]
        ring = sb("ring", [P, RING, PIECE])
        ident = sb("ident", [P, P])
        col = sb("col", [P, NCOLS])
        row = sb("row", [P, len(ROWS), H])
        mask8 = sb("mask8", [P, NG * T, S], U8)
        cond = sb("cond", [P, C, B])
        silu_cond = sb("silu_cond", [P, C, B])
        minus_half = sb("minus_half", [P, T])
        table_probe = sb("table_probe", [P, 1])
        scale = [[sb(f"scale{l}{w}", [P, C, B]) for w in range(2)] for l in range(2)]
        shift = [[sb(f"shift{l}{w}", [P, C, B]) for w in range(2)] for l in range(2)]
        xin = [sb(f"xin{s}", [P, T, H]) for s in "AB"]
        xres = [sb(f"xres{s}", [P, T, H]) for s in "AB"]
        xout = sb("xout", [P, T, H])
        gate_rows = xout[0:B, :, :]
        part = [sb(f"part{w}", [P, T, H]) for w in range(2)]
        gate = [sb(f"gate{w}", [P, T, H]) for w in range(2)]
        stats = [sb(f"stats{w}", [P, T, 6]) for w in range(2)]
        moments = [sb(f"moments{w}", [P, T, 2]) for w in range(2)]
        var_eps = [sb(f"var_eps{w}", [P, T]) for w in range(2)]
        rstd = [sb(f"rstd{w}", [P, T]) for w in range(2)]
        xn = [sb(f"xn{w}", [P, T, H]) for w in range(2)]
        mod = [sb(f"mod{w}", [P, C, G]) for w in range(2)]
        nrm = [[sb(f"nrm{w}{h}", [P, C, G], F32R) for h in ("hi", "lo")] for w in range(2)]
        maskf = sb("maskf", [P, T, S])
        qt = sb("qt", [P, C, G])
        kt = sb("kt", [P, C, G])
        kheads = sb("kheads", [P, C, HT, G])
        vt = sb("vt", [P, T, H])
        vswap = sb("vswap", [P, T, H])
        vpairs = sb("vpairs", [P, GB, NPAIR, PAIR])
        prob = sb("prob", [P, T, RT, C * HT, S])
        top = sb("top", [P, T, RT, C * HT])
        probt = sb("probt", [P, T, RT, 4, P])
        inv = sb("inv", [P, T, NH])
        yn = sb("yn", [P, T, H])
        yt = [sb(f"yt{h}", [P, C, G], F32R) for h in ("hi", "lo")]
        hid = sb("hid", [P, 2, 2, G])
        ht = [sb(f"ht{h}", [P, HC, G], F32R) for h in ("hi", "lo")]

        b_turn = bank("b_turn")
        b_mix = [bank("b_mix0"), bank("b_mix1")]
        b_score = [[bank(f"b_score{t}{r}") for r in range(RT)] for t in range(T)]
        b_hid = b_mix + [b_turn, b_mix[0]]
        b_y = [b_score[t][0] for t in range(T)]
        b_wo = b_score[0][1]
        b_yt = b_score[1][1]
        b_v = b_score[1][1]
        b_pt = [b_mix, [b_score[1][1], b_score[0][1]]]
        b_mlp = bank("b_mlp")

        names = """const_in xin_A xin_B gate_in0 gate_in1 gate_out out_stored piece_in0 piece_in1 piece_in2
            w_hi w_lo ada_mm ada_read pool_ready dve_ready silu
            stat0 aggr0 var0 rstd0 xn0 turned0 scaled0 mod0 hi0 lo0
            stat1 aggr1 var1 rstd1 xn1 turned1 scaled1 mod1 hi1 lo1 gelu_table
            q_mm k_mm v_mm q_done k_done kheads_dve kheads_act v_done v_swapped vpairs_done score_mm mask_ready masked topped shifted exp_done
            pt_mm pt_done pv_mm inv_done y_done y_turned y_hi y_lo wo_mm
            w1_mm h_f32 h_hi h_lo_pool h_lo_dve w2_mm
            gate_bias0 base0 gated0 res0 gate_bias1 base1 gated1 res1""".split()
        s = {n: ctx.enter_context(nc.semaphore(f"s_{n}")) for n in names}

        def await_unit(eng, name, u, back=0, per=1, k=1):
            if not u.static or u.index >= back:
                eng.wait_ge(s[name], per * (u.index - back) + k)

        def await_group(eng, name, u, back=0, per=1, k=1):
            if not u.static or u.group >= back:
                eng.wait_ge(s[name], per * (u.group - back) + k)

        def await_alone(eng, name, u, back=0, per=1, k=1):
            if not u.static or u.index >= back:
                eng.wait_ge(s[name], per * (u.index - back) + k)
                eng.nop(nofuse=True)

        def await_x(eng, u):
            eng.wait_ge(s["xin_" + "AB"[u.stream]], 16 * u.turn + 16)

        def c_(name, j):
            return col[:, COLS[name][0] + j:COLS[name][0] + j + 1]

        def row_all(name):
            return row[:, ROWS.index(name), :].unsqueeze(1).broadcast_to([P, T, H])

        def tokens(m, u):
            return m[:, :, bass.ds(u.group * GB, GB)].unsqueeze(3).broadcast_to([P, C, GB, S])

        def by_seq(ap):
            return ap.rearrange("p c (b s) -> p c b s", b=GB)

        def by_chunk(bk):
            return bk[:, :].rearrange("p (c n) -> p c n", c=2)

        def raw(ap):
            return ap.bitcast(F32)

        def split_parts(name):
            kind, l = name[:2], int(name[2])
            if kind == "qk":
                return [w[:, :, :].rearrange("p c n -> p (c n)") for w in wqk[l]]
            if kind == "vo":
                return [w[:, :, :].rearrange("p c n -> p (c n)") for w in wvo[l]]
            part_no = "ab".index(name[3])
            if kind == "w1":
                return [w[:, part_no].rearrange("p c n -> p (c n)") for w in w1[l]]
            half = HC // 2
            return [w[:, part_no * half:(part_no + 1) * half].rearrange("p c n -> p (c n)") for w in w2[l]]

        def await_piece(eng, name):
            n = PIECES.index(name)
            eng.wait_ge(s[f"piece_in{n % RING}"], 16 * (n // RING) + 16)

        def staged(name):
            return ring[:, PIECES.index(name) % RING, :]

        def chained(m):
            return m is not None and m.layer == 0

        def before(m):
            if m is None or (m.static and m.index == 0) or chained(Unit(m.r, m.c - 1)):
                return None
            return Unit(m.r, m.c - 1)

        def run_slots(eng, slot):
            slot(Unit(0, 0), None, Unit(0, 1))
            for q in range(1, 5):
                slot(Unit(0, q), Unit(0, q - 1), Unit(0, q + 1))
            with eng.Fori(1, ROUNDS) as i:
                for q in range(1, 5):
                    slot(Unit(i, q), Unit(i, q - 1), Unit(i, q + 1))
            for q in range(1, 4):
                slot(Unit(ROUNDS, q), Unit(ROUNDS, q - 1), Unit(ROUNDS, q + 1) if q < 3 else None)
            slot(None, Unit(ROUNDS, 3), None)

        block = ctx.enter_context(nc.Block())

        @block.sync
        def _(sp):
            def load_x(u):
                if not u.static or u.turn >= 1:
                    await_alone(sp, "xn0", u, back=4, per=T, k=T)
                    await_alone(sp, "base0", u, back=4)
                sp.dma_start(xin[u.stream][:, :, :], x_g[u.group]).then_inc(s["xin_" + "AB"[u.stream]], 16)

            def load_gate(w, u):
                await_group(sp, f"gated{w}", u, back=1)
                for half in range(2):
                    sp.dma_start(gate[w][64 * half:64 * half + 64, :, :],
                                 gates_g[u.group, w, half].partition_broadcast(64)).then_inc(s[f"gate_in{w}"], 16)

            def load_piece(n):
                if n >= RING:
                    old = PIECES[n - RING]
                    if old in ADAPTIVE:
                        sp.wait_ge(s["ada_mm"], ADAPTIVE.index(old) + 1)
                    else:
                        sp.wait_ge(s["w_hi"], SPLIT.index(old) + 1)
                        sp.wait_ge(s["w_lo"], SPLIT.index(old) + 1)
                sp.dma_start(ring[:, n % RING, :], pieces[n]).then_inc(s[f"piece_in{n % RING}"], 16)

            load_x(Unit(0, 0))
            sp.dma_start(ident[:, :], ident_in).then_inc(s["const_in"], 16)
            sp.dma_start(cond[:, :, :], cond_t.rearrange("(c p) b -> p c b", p=P)).then_inc(s["const_in"], 16)
            sp.dma_start(col[:, :], cols).then_inc(s["const_in"], 16)
            load_piece(0)
            load_piece(1)
            sp.dma_start(row[:, :, :], rows.partition_broadcast(P)).then_inc(s["const_in"], 16)
            for half in range(2):
                sp.dma_start(mask8[64 * half:64 * half + 64, :, :],
                             mask.rearrange("(t h) k -> h t k", h=2)[half].partition_broadcast(64))\
                  .then_inc(s["const_in"], 16)
            load_x(Unit(0, 1))
            for n in range(2, len(PIECES)):
                load_piece(n)
            sp.wait_ge(s["ada_read"], ADA_READS)
            sp.dma_start(gates_dram.rearrange("w b f -> b w f"), gate_rows[:, :, :]).then_inc(s["gate_out"], 16)
            sp.wait_ge(s["gate_out"], 16)

            def swap_values(u):
                await_unit(sp, "v_done", u)
                await_unit(sp, "vpairs_done", u, back=1, per=4, k=4)
                for half in range(2):
                    sp.dma_start(vswap[64 * half:64 * half + 64, :, :], vt[64 - 64 * half:128 - 64 * half, :, :])\
                      .then_inc(s["v_swapped"], 16)

            def store(u):
                await_alone(sp, "res1", u)
                sp.dma_start(out_g[u.group], xout[:, :, :]).then_inc(s["out_stored"], 16)

            def slot(a, m, nx):
                if a is not None and a.layer == 1:
                    load_gate(0, a)
                if a is not None:
                    swap_values(a)
                if before(m) is not None:
                    store(before(m))
                if m is not None and m.layer == 1:
                    load_gate(1, m)
                if a is None:
                    store(m)

            def round_(i):
                for q in range(1, 5):
                    if q in (2, 3):
                        load_x(Unit(i, q + 2))
                    slot(Unit(i, q), Unit(i, q - 1), Unit(i, q + 1))

            slot(Unit(0, 0), None, Unit(0, 1))
            round_(0)
            with sp.Fori(1, ROUNDS) as i:
                round_(i)
            for q in range(1, 4):
                slot(Unit(ROUNDS, q), Unit(ROUNDS, q - 1), None)
            slot(None, Unit(ROUNDS, 3), None)
            sp.wait_ge(s["out_stored"], 16 * NG)

        @block.tensor
        def _(pe):
            def product(o, n_k, lhs, rhs, moving=False, lo_wait=None):
                for k in range(n_k):
                    for weight in range(2):
                        pair = (weight, 0) if moving else (0, weight)
                        pe.matmul(o, lhs(k, pair[0]), rhs(k, pair[1]), start=(k == 0 and weight == 0), stop=False)
                if lo_wait is not None:
                    lo_wait()
                for k in range(n_k):
                    mm = pe.matmul(o, lhs(k, 0 if moving else 1), rhs(k, 1 if moving else 0), start=False,
                                   stop=(k == n_k - 1))
                return mm

            def out_products_hi(bk, n_k, x_, w, cols_, hi_wait):
                first = True
                for ks in (range(n_k - 2), range(n_k - 2, n_k)):
                    for t in range(T):
                        for k in ks:
                            hi_wait(t, k)
                            for weight in range(2):
                                pe.matmul(bk[:, t * H:(t + 1) * H], x_[0][:, k, t * P:(t + 1) * P],
                                          w[weight][:, k, cols_], start=first, stop=False)
                                first = False

            def out_products_lo(bk, n_k, x_, w, cols_, ts=range(T)):
                for t in ts:
                    for k in range(n_k):
                        mm = pe.matmul(bk[:, t * H:(t + 1) * H], x_[1][:, k, t * P:(t + 1) * P], w[0][:, k, cols_],
                                       start=False, stop=(t == T - 1 and k == n_k - 1))
                return mm

            def turn(src, bk):
                for t in range(T):
                    for c in range(C):
                        mm = pe.transpose(bk[:, c * G + t * P:c * G + (t + 1) * P],
                                          src[:, t, c * P:(c + 1) * P], ident[:, :])
                return mm

            def turn_norm0(u):
                await_unit(pe, "xn0", u, per=T, k=T)
                turn(xn[0], b_turn).then_inc(s["turned0"], 1)

            def adaptive(name):
                n = ADAPTIVE.index(name)
                await_piece(pe, name)
                if n:
                    pe.wait_ge(s["ada_read"], sum(READS[:n]))
                cc = cond if name in ("ada1", "ada2") else silu_cond
                w = staged(name).rearrange("p (c n) -> p c n", c=C)
                if cc is silu_cond:
                    pe.wait_ge(s["silu"], 1)
                for j in FEATURE_CHUNKS[name]:
                    for k in range(C):
                        mm = pe.matmul(b_mlp[:, j * B:(j + 1) * B], w[:, k, j * P:(j + 1) * P], cc[:, k, :],
                                       start=(k == 0), stop=(k == C - 1))
                if name in GATE_COLUMNS:
                    a = GATE_COLUMNS[name]
                    for k in range(C):
                        mm = pe.matmul(b_mlp[0:B, 256:512], cc[:, k, :], w[:, k, a:a + H],
                                       start=(k == 0), stop=(k == C - 1))
                mm.then_inc(s["ada_mm"], 1)

            def project(u):
                w, x_ = wqk[u.layer], nrm[0]
                await_unit(pe, "hi0", u)
                for which, name in ((1, "k_mm"), (0, "q_mm")):
                    await_unit(pe, "pt_done", u, back=1, per=4, k=which + 1)
                    for c in range(C):
                        a = which * H + c * P
                        mm = product(b_mix[which][:, c * G:(c + 1) * G], C, lambda k, h: w[h][:, k, a:a + P],
                                     lambda k, h: x_[h][:, k, :], moving=True,
                                     lo_wait=lambda: which == 1 and c == 0 and await_unit(pe, "lo0", u))
                    mm.then_inc(s[name], 1)
                if u.static and u.index == 0:
                    pe.wait_ge(s["w_lo"], SPLIT.index("vo0") + 1)
                await_unit(pe, "y_lo", u, back=1)
                for t in range(T):
                    mm = product(b_v[:, t * H:(t + 1) * H], C, lambda k, h: x_[h][:, k, t * P:(t + 1) * P],
                                 lambda k, h: wvo[u.layer][h][:, k, 0:H])
                mm.then_inc(s["v_mm"], 1)

            def scores(u, t, r):
                if t == 0 and r == 0:
                    await_alone(pe, "q_done", u, per=C, k=C)
                    await_alone(pe, "kheads_act", u)
                    await_alone(pe, "kheads_dve", u, per=HT - 1, k=HT - 1)
                if t == 1 and r == 1:
                    await_alone(pe, "v_done", u)
                rows_ = slice(64 * r, 64 * r + 64)
                for c in range(C):
                    for j in range(2):
                        b = slice((2 * t + j) * S, (2 * t + j + 1) * S)
                        mm = pe.matmul(b_score[t][r][64 * j:64 * j + 64, c * HT * S:(c + 1) * HT * S],
                                       qt[rows_, c, b], kheads[rows_, c, :, b], start=True, stop=True)
                mm.then_inc(s["score_mm"], 1)

            def turn_norm1(u):
                await_unit(pe, "xn1", u, per=T, k=T)
                turn(xn[1], b_turn).then_inc(s["turned1"], 1)

            def hidden(u, a):
                w = w1[u.layer]
                await_unit(pe, "hi1", u)
                for jp in range(HP):
                    if jp == 3:
                        await_unit(pe, "h_f32", u, per=HC, k=2)
                    elif jp == 2:
                        await_unit(pe, "mod1", u)
                    elif a is not None:
                        await_unit(pe, ("q_done", "k_done")[jp], a, per=C, k=C)
                    else:
                        await_unit(pe, "pt_done", u, per=4, k=jp + 1)
                    for e in range(2):
                        j = 2 * jp + e
                        hc = slice(j % 4 * P, j % 4 * P + P)
                        mm = product(b_hid[jp][:, e * G:(e + 1) * G],
                                     C, lambda k, h: w[h][:, j // 4, k, hc], lambda k, h: nrm[1][h][:, k, :],
                                     moving=True, lo_wait=lambda: j == 0 and await_unit(pe, "lo1", u))
                    mm.then_inc(s["w1_mm"], 1)

            def mlp_out_hi(u):
                await_unit(pe, "res1", u, back=1)

                def hidden_hi(t, k):
                    if t == 0 and k % 2 == 0:
                        await_unit(pe, "h_hi", u, per=HP, k=k // 2 + 1)

                out_products_hi(b_mlp, HC, ht, w2[u.layer], slice(0, H), hidden_hi)

            def mlp_out_lo(u, ts=range(T)):
                await_unit(pe, "h_lo_pool", u, per=HP // 2, k=HP // 2)
                await_unit(pe, "h_lo_dve", u, per=HP // 2, k=HP // 2)
                mm = out_products_lo(b_mlp, HC, ht, w2[u.layer], slice(0, H), ts)
                if ts[-1] == T - 1:
                    mm.then_inc(s["w2_mm"], 1)

            def turn_probs(u, m, t):
                for r in range(RT):
                    await_unit(pe, "exp_done", u, per=4, k=r + 1 if t == 0 else 4)
                    if t == 0 and m is not None:
                        await_unit(pe, "h_f32", m, per=HC, k=(8, 4)[r])
                    elif t == 0:
                        await_unit(pe, ("q_done", "k_done")[r], u, per=C, k=C)
                    for q in range(4):
                        mm = pe.transpose(b_pt[t][r][:, q * P:(q + 1) * P],
                                          prob[:, t, r, 2 * q:2 * q + 2, :].rearrange("p h k -> p (h k)"), ident[:, :])
                    mm.then_inc(s["pt_mm"], 1)

            def values(u, t):
                for r in range(RT):
                    if t == 0 and r == 0:
                        await_alone(pe, "vpairs_done", u, per=4, k=4)
                    await_alone(pe, "pt_done", u, per=4, k=2 * t + r + 1)
                    for q in range(4):
                        pair = 4 * (q // 2) + 2 * r + q % 2
                        for j in range(2):
                            mm = pe.matmul(b_y[t][64 * j:64 * j + 64, pair * PAIR:(pair + 1) * PAIR],
                                           probt[:, t, r, q, 64 * j:64 * j + 64], vpairs[:, 2 * t + j, pair, :],
                                           start=True, stop=True)
                mm.then_inc(s["pv_mm"], 1)

            def turn_y(u):
                await_unit(pe, "y_done", u, per=T, k=T)
                turn(yn, b_yt).then_inc(s["y_turned"], 1)

            def attention_out(u):
                await_unit(pe, "y_hi", u)
                out_products_hi(b_wo, C, yt, wvo[u.layer], slice(H, 2 * H), lambda t, k: None)
                await_unit(pe, "y_lo", u)
                out_products_lo(b_wo, C, yt, wvo[u.layer], slice(H, 2 * H)).then_inc(s["wo_mm"], 1)

            pe.wait_ge(s["const_in"], 16 * CONSTS)
            turn_norm0(Unit(0, 0))
            adaptive("ada1")

            def slot(a, m, nx):
                first = m is None
                if a is not None:
                    if first:
                        pe.wait_ge(s["w_lo"], SPLIT.index("qk0") + 1)
                    project(a)
                    scores(a, 0, 0)
                if m is not None:
                    turn_norm1(m)
                if a is not None:
                    scores(a, 0, 1)
                    scores(a, 1, 0)
                    scores(a, 1, 1)
                if m is not None:
                    hidden(m, a)
                    mlp_out_hi(m)
                    if chained(m) or a is None:
                        mlp_out_lo(m)
                if first:
                    for name in ADAPTIVE[1:]:
                        adaptive(name)

                def turn_next():
                    if nx is not None:
                        if m is None:
                            await_unit(pe, "mod0", a)
                        else:
                            await_unit(pe, "h_f32", m, per=HC, k=6)
                        turn_norm0(nx)

                if a is not None:
                    late = m is not None and not chained(m)
                    if late:
                        mlp_out_lo(m, [0])
                    turn_probs(a, m, 0)
                    turn_probs(a, m, 1)
                    values(a, 0)
                    values(a, 1)
                    turn_next()
                    turn_y(a)
                    if late:
                        mlp_out_lo(m, [1])
                    attention_out(a)
                if first:
                    pe.wait_ge(s["w_lo"], len(SPLIT))

            run_slots(pe, slot)

        @block.scalar
        def _(act):
            def split_hi(name):
                await_piece(act, name)
                act.activation(split_parts(name)[0], staged(name), ACT.Copy).then_inc(s["w_hi"], 1)

            def norm_hi(w, u):
                await_unit(act, f"mod{w}", u)
                if w == 1:
                    await_unit(act, "w1_mm", u, back=1, per=HP, k=HP)
                else:
                    await_unit(act, "v_mm", u, back=1)
                act.activation(nrm[w][0][:, :, :], mod[w][:, :, :], ACT.Copy).then_inc(s[f"hi{w}"], 1)

            act.wait_ge(s["const_in"], 16 * CONSTS)
            act.activation(silu_cond[:, :, :], cond[:, :, :], ACT.Silu).then_inc(s["silu"], 1)
            for name in PIECES[:EARLY]:
                if name in SPLIT:
                    split_hi(name)
            norm_hi(0, Unit(0, 0))

            def slot(a, m, nx):
                if a is not None:
                    for name, dst in (("k", kt), ("q", qt)):
                        await_unit(act, f"{name}_mm", a)
                        if name == "q":
                            await_unit(act, "score_mm", a, back=1, per=4, k=4)
                        else:
                            await_unit(act, "kheads_dve", a, back=1, per=HT - 1, k=HT - 1)
                        for c in range(C):
                            act.activation(dst[:, c, :], b_mix["qk".index(name)][:, c * G:(c + 1) * G], ACT.Identity,
                                           bias=c_(f"b{name}{a.layer}", c)).then_inc(s[f"{name}_done"], 1)
                        if name == "k":
                            await_unit(act, "k_done", a, per=C, k=C)
                            await_unit(act, "score_mm", a, back=1, per=4, k=4)
                            act.activation(kheads[:, :, HT - 1, :], kt[:, :, :], ACT.Copy, scale=c_("head", HT - 1))\
                               .then_inc(s["kheads_act"], 1)
                if m is not None:
                    norm_hi(1, m)
                    await_unit(act, "w2_mm", m, back=1)
                    for jp in range(HP):
                        await_unit(act, "w1_mm", m, per=HP, k=jp + 1)
                        taken = ("h_lo_pool", "h_lo_dve")[jp % 2]
                        if jp >= 2:
                            await_unit(act, taken, m, per=HP // 2, k=1)
                        else:
                            await_unit(act, taken, m, back=1, per=HP // 2, k=HP // 2)
                        for e in range(2):
                            j = 2 * jp + e
                            act.activation(hid[:, jp % 2, e, :], b_hid[jp][:, e * G:(e + 1) * G], ACT.Gelu,
                                           bias=c_(f"b1{m.layer}", j)).then_inc(s["h_f32"], 1)
                        await_unit(act, "h_f32", m, per=HC, k=2 * jp + 2)
                        act.activation(ht[0][:, 2 * jp:2 * jp + 2, :], hid[:, jp % 2], ACT.Copy).then_inc(s["h_hi"], 1)
                else:
                    for name in PIECES[EARLY:]:
                        if name in SPLIT:
                            split_hi(name)
                if a is not None:
                    for t in range(T):
                        for r in range(RT):
                            await_unit(act, "shifted", a, per=4, k=2 * t + r + 1)
                            act.activation(prob[:, t, r], prob[:, t, r], ACT.Exp, scale=SCORE_SCALE[a.layer])\
                               .then_inc(s["exp_done"], 1)
                    for t in range(T):
                        for r in range(RT):
                            await_unit(act, "pt_mm", a, per=4, k=2 * t + r + 1)
                            await_unit(act, "pv_mm", a, back=1, per=T, k=T)
                            act.activation(probt[:, t, r], b_pt[t][r][:, :].rearrange("p (q n) -> p q n", q=4), ACT.Copy)\
                               .then_inc(s["pt_done"], 1)
                    await_unit(act, "y_turned", a)
                    await_unit(act, "wo_mm", a, back=1)
                    act.activation(yt[0][:, :, :], by_chunk(b_yt), ACT.Copy).then_inc(s["y_hi"], 1)
                    if nx is not None:
                        norm_hi(0, nx)
                    await_unit(act, "gelu_table", a, back=1)
                    act.activation(table_probe[:, :], col[:, 0:1], ACT.Gelu).then_inc(s["gelu_table"], 1)

            run_slots(act, slot)

        @block.vector
        def _(dve):
            def split_lo(name):
                dve.wait_ge(s["w_hi"], SPLIT.index(name) + 1)
                hi, lo = split_parts(name)
                dve.tensor_tensor(lo, staged(name), raw(hi), ALU.subtract).then_inc(s["w_lo"], 1)

            def adaptive(name):
                n = ADAPTIVE.index(name)
                dve.wait_ge(s["ada_mm"], n + 1)
                for j, (dst, chunk, plus) in FEATURE_TARGETS(name, scale, shift).items():
                    dve.tensor_scalar(dst[:, chunk, :], b_mlp[:, j * B:(j + 1) * B], c_(name, j), plus,
                                      ALU.add, ALU.add).then_inc(s["ada_read"], 1)
                if name in GATE_COLUMNS:
                    w = 0 if name == "c1" else 1
                    dve.tensor_tensor(gate_rows[:, w, :], b_mlp[0:B, 256:512], row[0:B, ROWS.index(f"bg{w}"), :],
                                      ALU.add).then_inc(s["ada_read"], 1)

            def stats_of(w, u, src):
                for t in range(T):
                    dve.bn_stats(stats[w][:, t, :], src[:, t, :]).then_inc(s[f"stat{w}"], 1)

            def variance_of(w, u):
                await_alone(dve, f"stat{w}", u, per=T, k=T)
                for t in range(T):
                    dve.bn_aggr(moments[w][:, t, :], stats[w][:, t, :]).then_inc(s[f"aggr{w}"], 1)
                await_unit(dve, f"aggr{w}", u, per=T, k=T)
                dve.tensor_scalar(var_eps[w][:, :], moments[w][:, :, 1], EPS, None, ALU.add).then_inc(s[f"var{w}"], 1)

            def normed(w, u, src):
                await_unit(dve, f"rstd{w}", u)
                await_unit(dve, f"turned{w}", u, back=1)
                for t in range(T):
                    dve.tensor_scalar(xn[w][:, t, :], src[:, t, :], moments[w][:, t, 0:1], rstd[w][:, t:t + 1],
                                      ALU.subtract, ALU.mult).then_inc(s[f"xn{w}"], 1)

            def source(u):
                return xin[u.stream] if u.layer == 0 else xres[u.stream]

            def modulate(w, u):
                await_unit(dve, f"turned{w}", u)
                await_unit(dve, f"lo{w}", u, back=1)
                dve.tensor_tensor(by_seq(mod[w][:, :, :]), by_seq(by_chunk(b_turn)), tokens(scale[u.layer][w], u),
                                  ALU.mult).then_inc(s[f"scaled{w}"], 1)
                await_unit(dve, f"scaled{w}", u)
                dve.tensor_tensor(by_seq(mod[w][:, :, :]), by_seq(mod[w][:, :, :]), tokens(shift[u.layer][w], u),
                                  ALU.add).then_inc(s[f"mod{w}"], 1)

            def norm_lo(w, u):
                await_unit(dve, f"hi{w}", u)
                dve.tensor_tensor(nrm[w][1][:, :, :], mod[w][:, :, :], raw(nrm[w][0][:, :, :]), ALU.subtract)\
                   .then_inc(s[f"lo{w}"], 1)

            def residual(w, u, bk):
                await_unit(dve, ("wo_mm", "w2_mm")[w], u)
                last = w == 1 and u.layer == 1
                dst = (xout if last else xres[u.stream])[:, :, :]
                product = by_chunk(bk)
                if u.layer == 1:
                    dve.wait_ge(s[f"gate_in{w}"], 32 * u.group + 32)
                    if last and not (u.static and u.group == 0):
                        dve.wait_ge(s["out_stored"], 16 * u.group)
                    await_unit(dve, f"base{w}", u)
                    dve.tensor_tensor(dst, product, gate[w][:, :, :], ALU.mult).then_inc(s[f"gated{w}"], 1)
                    await_group(dve, f"gated{w}", u)
                    product = dst
                else:
                    await_unit(dve, f"base{w}", u)
                dve.tensor_tensor(dst, product, part[w][:, :, :], ALU.add).then_inc(s[f"res{w}"], 1)

            def pair_values(u, swapped):
                if swapped:
                    await_unit(dve, "v_swapped", u, per=32, k=32)
                else:
                    await_unit(dve, "v_done", u)
                    await_unit(dve, "pv_mm", u, back=1, per=T, k=T)
                for odd in range(2):
                    half = slice(64 * odd, 64 * odd + 64)
                    src = (vt, vswap)[swapped][half, :, :].rearrange("p t (n o d) -> p t n o d", n=NPAIR, o=2)
                    dve.tensor_copy(vpairs[half, odd ^ swapped:GB:2, :, odd * (HD + 1):odd * (HD + 1) + HD],
                                    src[:, :, :, odd, :]).then_inc(s["vpairs_done"], 1)

            def softmax(u, t, rs=range(RT)):
                for r in rs:
                    k = 2 * t + r + 1
                    src = b_score[t][r][:, :].rearrange("p (h k) -> p h k", h=C * HT)
                    dst = prob[:, t, r]
                    await_unit(dve, "score_mm", u, per=4, k=k)
                    await_unit(dve, "pt_mm", u, back=1, per=4, k=4)
                    if u.layer == 0:
                        dve.tensor_tensor(dst, src, maskf[:, t, :].unsqueeze(1).broadcast_to([P, C * HT, S]),
                                          ALU.add).then_inc(s["masked"], 1)
                        await_group(dve, "masked", u, per=4, k=k)
                        src = dst
                    dve.tensor_reduce(top[:, t, r, :], src, AX.X, ALU.max).then_inc(s["topped"], 1)
                    await_unit(dve, "topped", u, per=4, k=k)
                    dve.tensor_tensor(dst, src, top[:, t, r, :].unsqueeze(2).broadcast_to([P, C * HT, S]),
                                      ALU.subtract).then_inc(s["shifted"], 1)

            dve.memset(vpairs[:, :, :, :], 0.0).then_inc(s["dve_ready"], 1)
            dve.wait_ge(s["dve_ready"], 1)
            dve.memset(vpairs[0:64, :, :, HD:HD + 1], 1.0).then_inc(s["dve_ready"], 1)
            dve.memset(vpairs[64:128, :, :, PAIR - 1:PAIR], 1.0).then_inc(s["dve_ready"], 1)
            dve.wait_ge(s["dve_ready"], 3)
            dve.wait_ge(s["const_in"], 16 * CONSTS)
            await_x(dve, Unit(0, 0))
            stats_of(0, Unit(0, 0), xin[0])
            variance_of(0, Unit(0, 0))
            normed(0, Unit(0, 0), xin[0])
            adaptive("ada1")
            dve.wait_ge(s["ada_read"], READS[0])
            modulate(0, Unit(0, 0))
            split_lo("qk0")
            split_lo("vo0")
            norm_lo(0, Unit(0, 0))

            def lo_of_hidden(jp, u):
                await_unit(dve, "h_hi", u, per=HP, k=jp + 1)
                if jp == 1:
                    await_unit(dve, "w2_mm", u, back=1)
                dve.tensor_tensor(ht[1][:, 2 * jp:2 * jp + 2, :], hid[:, jp % 2], raw(ht[0][:, 2 * jp:2 * jp + 2, :]),
                                  ALU.subtract).then_inc(s["h_lo_dve"], 1)

            def slot(a, m, nx):
                if a is not None:
                    await_unit(dve, "k_done", a, per=C, k=C)
                    await_unit(dve, "score_mm", a, back=1, per=4, k=4)
                    for j in range(HT - 1):
                        dve.tensor_scalar(kheads[:, :, j, :], kt[:, :, :], c_("head", j), None, ALU.mult)\
                           .then_inc(s["kheads_dve"], 1)
                if m is not None:
                    normed(1, m, xres[m.stream])
                if a is not None:
                    await_unit(dve, "v_mm", a)
                    await_unit(dve, "vpairs_done", a, back=1, per=4, k=4)
                    dve.tensor_tensor(vt[:, :, :], by_chunk(b_v), row_all(f"bv{a.layer}"), ALU.add)\
                       .then_inc(s["v_done"], 1)
                if m is not None:
                    modulate(1, m)
                if a is not None:
                    pair_values(a, 0)
                    if a.layer == 0:
                        await_group(dve, "masked", a, back=1, per=4, k=4)
                        dve.tensor_scalar(maskf[:, :, :], mask8[:, bass.ds(a.group * T, T), :], -BIG, BIG,
                                          ALU.mult, ALU.mult).then_inc(s["mask_ready"], 1)
                        await_group(dve, "mask_ready", a)
                if m is not None:
                    norm_lo(1, m)
                if before(m) is not None:
                    residual(1, before(m), b_mlp)
                if a is not None:
                    softmax(a, 0)
                if m is not None:
                    lo_of_hidden(1, m)
                if a is not None:
                    softmax(a, 1, [0])
                if m is not None:
                    lo_of_hidden(3, m)
                if a is not None:
                    softmax(a, 1, [1])
                early = nx is not None and not chained(m)
                if early:
                    await_x(dve, nx)
                    stats_of(0, nx, source(nx))
                    variance_of(0, nx)
                if m is not None:
                    if a is not None:
                        pair_values(a, 1)
                    if chained(m) or a is None:
                        residual(1, m, b_mlp)
                else:
                    for name in PIECES[3:]:
                        if name in SPLIT:
                            split_lo(name)
                        else:
                            adaptive(name)
                    dve.wait_ge(s["ada_read"], ADA_READS)
                    pair_values(a, 1)

                def take_y(t):
                    sums = b_y[t][:, 0:NPAIR * PAIR].rearrange("p (h n) -> p h n", h=NH)
                    await_unit(dve, "pv_mm", a, per=T, k=t + 1)
                    dve.reciprocal(inv[:, t, :], sums[:, :, HD]).then_inc(s["inv_done"], 1)
                    await_unit(dve, "inv_done", a, per=T, k=t + 1)
                    await_unit(dve, "y_turned", a, back=1)
                    dve.tensor_tensor(yn[:, t, :].rearrange("p (h d) -> p h d", h=NH), sums[:, :, 0:HD],
                                      inv[:, t, :].unsqueeze(2).broadcast_to([P, NH, HD]), ALU.mult)\
                       .then_inc(s["y_done"], 1)

                if a is None:
                    return
                if early:
                    normed(0, nx, source(nx))
                elif nx is not None:
                    await_unit(dve, "res1", m)
                    stats_of(0, nx, source(nx))
                    variance_of(0, nx)
                    normed(0, nx, source(nx))
                take_y(0)
                take_y(1)
                if nx is not None:
                    modulate(0, nx)
                await_unit(dve, "y_hi", a)
                dve.tensor_tensor(yt[1][:, :, :], by_chunk(b_yt), raw(yt[0][:, :, :]), ALU.subtract)\
                   .then_inc(s["y_lo"], 1)
                if nx is not None:
                    norm_lo(0, nx)
                residual(0, a, b_wo)
                await_unit(dve, "res0", a)
                stats_of(1, a, xres[a.stream])
                variance_of(1, a)

            run_slots(dve, slot)

        @block.gpsimd
        def _(pool):
            def inverse_root(w, u):
                await_unit(pool, f"var{w}", u)
                pool.tensor_tensor(rstd[w][:, :], var_eps[w][:, :], minus_half[:, :], ALU.pow).then_inc(s[f"rstd{w}"], 1)

            def base(w, u, src):
                await_unit(pool, f"res{w}", u, back=1)
                bias = row_all(ROW_OF[w] + str(u.layer))
                if u.layer == 1:
                    pool.wait_ge(s[f"gate_in{w}"], 32 * u.group + 32)
                    pool.tensor_tensor(part[w][:, :, :], gate[w][:, :, :], bias, ALU.mult).then_inc(s[f"gate_bias{w}"], 1)
                    await_group(pool, f"gate_bias{w}", u)
                    bias = part[w][:, :, :]
                pool.tensor_tensor(part[w][:, :, :], src[:, :, :], bias, ALU.add).then_inc(s[f"base{w}"], 1)

            pool.memset(minus_half[:, :], -0.5).then_inc(s["pool_ready"], 1)
            pool.wait_ge(s["pool_ready"], 1)
            inverse_root(0, Unit(0, 0))
            pool.wait_ge(s["const_in"], 16 * CONSTS)

            def slot(a, m, nx):
                if m is not None:
                    inverse_root(1, m)
                if a is not None:
                    if a.layer == 0:
                        await_x(pool, a)
                    else:
                        await_unit(pool, "res1", a, back=2)
                    base(0, a, xin[a.stream] if a.layer == 0 else xres[a.stream])
                if m is not None:
                    if chained(m):
                        await_unit(pool, "res0", m)
                        base(1, m, xres[m.stream])
                    for jp in (0, 2):
                        await_unit(pool, "h_hi", m, per=HP, k=jp + 1)
                        if jp == 0:
                            await_unit(pool, "w2_mm", m, back=1)
                        pool.tensor_tensor(ht[1][:, 2 * jp:2 * jp + 2, :], hid[:, jp % 2], raw(ht[0][:, 2 * jp:2 * jp + 2, :]),
                                           ALU.subtract).then_inc(s["h_lo_pool"], 1)
                if nx is not None:
                    inverse_root(0, nx)
                if m is not None and not chained(m):
                    await_unit(pool, "res0", m)
                    base(1, m, xres[m.stream])

            run_slots(pool, slot)


ROW_OF = ("bo", "b2")
FEATURE_CHUNKS = {"ada1": range(4), "ada2": range(4), "c0": range(4), "c1": (2, 3), "c2": (0, 1)}
GATE_COLUMNS = {"c1": 0, "c2": H}
READS = [len(FEATURE_CHUNKS[n]) + (n in GATE_COLUMNS) for n in ADAPTIVE]
ADA_READS = sum(READS)
CONSTS = 6


def FEATURE_TARGETS(name, scale, shift):
    one, none = (scale, 1.0), (shift, 0.0)
    parts = {"ada1": {0: (one, 0, 0), 2: (none, 0, 0)}, "ada2": {0: (one, 0, 1), 2: (none, 0, 1)},
             "c0": {0: (none, 1, 0), 2: (one, 1, 0)}, "c1": {2: (none, 1, 1)}, "c2": {0: (one, 1, 1)}}[name]
    return {j + c: (kind[0][l][w], c, kind[1]) for j, (kind, l, w) in parts.items() for c in range(C)}


def kernel(x, cond_1024, mask_BxS_bf0, **w):
    import concourse.bacc as bacc
    from concourse.bass_utils import run_bass_kernel_spmd as run

    w = {k: np.asarray(v) for k, v in w.items()}

    def wide(m):
        return m.reshape(C, P, 2 * H).transpose(1, 0, 2).reshape(P, PIECE)

    def tall(m):
        return m.reshape(HC // 2, P, H).transpose(1, 0, 2).reshape(P, PIECE)

    L0 = {n: w[f"L0_cond_{n}"].T for n in ("w_adaln1", "w_adaln2", "wq", "wk", "wv", "wo", "w1", "w2")}
    L1 = {n.lower(): w[f"L1_cond_{n}"] for n in ("Wc", "Wq", "Wk", "Wv", "Wo", "W1", "W2")}
    pieces = {"ada1": wide(L0["w_adaln1"]), "ada2": wide(L0["w_adaln2"])}
    for j in range(3):
        pieces[f"c{j}"] = wide(L1["wc"][:, j * 512:(j + 1) * 512])
    for l, m in enumerate((L0, L1)):
        pieces[f"qk{l}"] = wide(np.concatenate([m["wq"], m["wk"]], 1))
        pieces[f"vo{l}"] = wide(np.concatenate([m["wv"], m["wo"]], 1))
        for j, h in enumerate("ab"):
            pieces[f"w1{l}{h}"] = wide(m["w1"][:, j * 512:(j + 1) * 512])
            pieces[f"w2{l}{h}"] = tall(m["w2"][j * 512:(j + 1) * 512])
    pieces = np.stack([pieces[n] for n in PIECES])

    def by_column(v):
        return v.reshape(-1, P).T

    bc = w["L1_cond_bc"]
    head = (np.arange(P)[:, None] % 64 // HD == np.arange(HT)[None, :]).astype(np.float32)
    cols = {"bq0": w["L0_cond_bq"], "bk0": w["L0_cond_bk"], "bq1": w["L1_cond_bq"], "bk1": w["L1_cond_bk"],
            "b10": w["L0_cond_b1"], "b11": w["L1_cond_b1"], "ada1": w["L0_cond_b_adaln1"],
            "ada2": w["L0_cond_b_adaln2"], "c0": bc[0:512], "c1": bc[512:1024], "c2": bc[1024:1536]}
    cols = np.concatenate([by_column(cols[n]) if n != "head" else head for n in COLS], 1)
    rows = {"bv0": w["L0_cond_bv"], "bo0": w["L0_cond_bo"], "b20": w["L0_cond_b2"], "bv1": w["L1_cond_bv"],
            "bo1": w["L1_cond_bo"], "b21": w["L1_cond_b2"], "bg0": bc[512:768], "bg1": bc[1280:1536]}
    rows = np.stack([rows[n] for n in ROWS])
    arrays = {"x": np.asarray(x), "cond_t": np.asarray(cond_1024).T, "mask": np.asarray(mask_BxS_bf0),
              "pieces": pieces, "cols": cols, "rows": rows, "ident": np.eye(P, dtype=np.float32)}
    arrays = {f"in_{k}": np.ascontiguousarray(v) for k, v in arrays.items()}

    nc = bacc.Bacc("TRN2", target_bir_lowering=False, num_devices=1, dynamic_dma_scratch_size=1024)
    aps = [nc.dram_tensor(k, v.shape, mybir.dt.from_np(v.dtype), kind="ExternalInput").ap() for k, v in arrays.items()]
    out = nc.dram_tensor("out", (B, S, H), F32, kind="ExternalOutput").ap()
    build(nc, *aps, out)
    return run(nc, [arrays], core_ids=[0]).results[0]["out"]
```

```python
from contextlib import ExitStack

import numpy as np
import concourse.bass as bass
from concourse import mybir
from concourse.alu_op_type import AluOpType as ALU

ACT = mybir.ActivationFunctionType
AX = mybir.AxisListType
F32 = mybir.dt.float32
F32R = mybir.dt.float32r
U8 = mybir.dt.uint8

P = 128
B, S, H = 64, 64, 256
NH = 16
HD = H // NH
MLP = 1024
EPS = 1e-5
GB = 4
G = GB * S
T = G // P
C = H // P
NG = B // GB
HC = MLP // P
HP = HC // 2
ROUNDS = NG // 2 - 1
HT = 4
RT = 2
PAIR = 2 * (HD + 1)
NPAIR = NH // 2
SCORE_SCALE = (HD ** -0.5, 1.0 / HD)
BIG = 3e38

PIECES = ["ada1", "qk0", "vo0", "ada2", "w10a", "w10b", "w20a", "w20b",
          "c0", "c1", "c2", "qk1", "vo1", "w11a", "w11b", "w21a", "w21b"]
ADAPTIVE = ["ada1", "ada2", "c0", "c1", "c2"]
SPLIT = [n for n in PIECES if n not in ADAPTIVE]
SPLIT_DVE = ["qk0", "vo0", "w10b"]
SPLIT_POOL = [n for n in SPLIT if n not in SPLIT_DVE]
PIECE = 1024
RING = 3
FIRST = 8
SPLIT_LATE = {1: ["qk1", "vo1", "w11a"], 2: ["w11b"], 3: ["w21a", "w21b"]}
COLS, NCOLS = {}, 0
for _name, _n in (("bq0", C), ("bk0", C), ("bq1", C), ("bk1", C), ("b10", HC), ("b11", HC),
                  ("ada1", 4), ("ada2", 4), ("c0", 4), ("c1", 4), ("c2", 4), ("head", HT)):
    COLS[_name] = (NCOLS, _n)
    NCOLS += _n
ROWS = ["bv0", "bo0", "b20", "bv1", "bo1", "b21", "bg0", "bg1"]


class Unit:

    def __init__(self, r, c):
        self.r, self.c = r, c
        self.static = isinstance(r, int)
        self.index = 4 * r + c
        self.layer = c % 4 // 2
        self.stream = c % 2
        self.turn = r + c // 4
        self.group = 2 * r + 2 * (c // 4) + c % 2


def build(nc, x, cond_t, mask, pieces, cols, rows, ident_in, out):
    ctx = ExitStack()
    with ctx:
        def sb(name, shape, dt=F32):
            return ctx.enter_context(nc.sbuf_tensor(name, shape, dt))

        def bank(name):
            return ctx.enter_context(nc.psum_tensor(name, [P, 512], F32))

        x_g = x.rearrange("b s f -> (b s) f").rearrange("(g t p) f -> g p t f", t=T, p=P)
        out_g = out.rearrange("b s f -> (b s) f").rearrange("(g t p) f -> g p t f", t=T, p=P)
        gates_dram = nc.dram_tensor("gates_dram", [2, B, H], F32, kind="Internal").ap()
        gates_g = gates_dram.rearrange("w (g t h) f -> g w h t f", t=T, h=2)

        wqk = [[sb(f"wqk{l}{h}", [P, C, 2 * H], F32R) for h in ("hi", "lo")] for l in range(2)]
        wvo = [[sb(f"wvo{l}{h}", [P, C, 2 * H], F32R) for h in ("hi", "lo")] for l in range(2)]
        w1 = [[sb(f"w1{l}{h}", [P, 2, C, MLP // 2], F32R) for h in ("hi", "lo")] for l in range(2)]
        w2 = [[sb(f"w2{l}{h}", [P, HC, H], F32R) for h in ("hi", "lo")] for l in range(2)]
        ring = sb("ring", [P, RING, PIECE])
        ident = sb("ident", [P, P])
        col = sb("col", [P, NCOLS])
        row = sb("row", [P, len(ROWS), H])
        mask8 = sb("mask8", [P, NG * T, S], U8)
        cond = sb("cond", [P, C, B])
        silu_cond = sb("silu_cond", [P, C, B])
        minus_half = sb("minus_half", [P, T])
        table_probe = sb("table_probe", [P, 1])
        scale = [[sb(f"scale{l}{w}", [P, C, B]) for w in range(2)] for l in range(2)]
        shift = [[sb(f"shift{l}{w}", [P, C, B]) for w in range(2)] for l in range(2)]
        xin = [sb(f"xin{s}", [P, T, H]) for s in "AB"]
        xres = [sb(f"xres{s}", [P, T, H]) for s in "AB"]
        xout = sb("xout", [P, T, H])
        gate_rows = xout[0:B, :, :]
        part = [sb(f"part{w}", [P, T, H]) for w in range(2)]
        gate = [sb(f"gate{w}", [P, T, H]) for w in range(2)]
        stats = [sb(f"stats{w}", [P, T, 6]) for w in range(2)]
        moments = [sb(f"moments{w}", [P, T, 2]) for w in range(2)]
        var_eps = [sb(f"var_eps{w}", [P, T]) for w in range(2)]
        rstd = [sb(f"rstd{w}", [P, T]) for w in range(2)]
        xn = [sb(f"xn{w}", [P, T, H]) for w in range(2)]
        mod = [sb(f"mod{w}", [P, C, G]) for w in range(2)]
        nrm = [[sb(f"nrm{w}{h}", [P, C, G], F32R) for h in ("hi", "lo")] for w in range(2)]
        maskf = sb("maskf", [P, T, S])
        qt = sb("qt", [P, C, G])
        kt = sb("kt", [P, C, G])
        kheads = sb("kheads", [P, C, HT, G])
        vt = sb("vt", [P, T, H])
        vswap = sb("vswap", [P, T, H])
        vpairs = sb("vpairs", [P, GB, NPAIR, PAIR])
        prob = sb("prob", [P, T, RT, C * HT, S])
        top = sb("top", [P, T, RT, C * HT])
        probt = sb("probt", [P, T, RT, 4, P])
        inv = sb("inv", [P, T, NH])
        yn = sb("yn", [P, T, H])
        yt = [sb(f"yt{h}", [P, C, G], F32R) for h in ("hi", "lo")]
        hid = sb("hid", [P, 2, 2, G])
        ht = [sb(f"ht{h}", [P, HC, G], F32R) for h in ("hi", "lo")]

        b_turn = bank("b_turn")
        b_mix = [bank("b_mix0"), bank("b_mix1")]
        b_score = [[bank(f"b_score{t}{r}") for r in range(RT)] for t in range(T)]
        b_hid = b_mix + [b_turn, b_mix[0]]
        b_y = [b_score[t][0] for t in range(T)]
        b_wo = b_score[0][1]
        b_yt = [b_score[1][1], b_mix[0]]
        b_v = b_score[1][1]
        b_pt = [b_mix, [b_score[1][1], b_score[0][1]]]
        b_mlp = bank("b_mlp")

        names = """const_in xin_A xin_B gate_in0 gate_in1 gate_out out_stored piece_in0 piece_in1 piece_in2
            piece_in3 piece_in4 piece_in5 piece_in6 piece_in7 rows_in w_hi w_lo_pool w_lo_dve
            ada_mm ada_read pool_ready dve_ready silu gelu_table
            stat0 aggr0 var0 rstd0 xn0 turned0 scaled0 mod0 hi0 lo0
            stat1 aggr1 var1 rstd1 xn1 turned1 scaled1 mod1 hi1 lo1
            q_mm k_mm v_mm q_done k_done kheads_dve kheads_act v_done v_swapped vpairs_done
            score_mm mask_ready masked topped shifted exp_done
            pt_mm pt_done pv_mm inv_done y_done y_turned y_hi y_lo wo_mm
            w1_mm h_f32 h_hi h_lo_pool h_lo_dve w2_mm
            gate_bias0 base0 gated0 res0 gate_bias1 base1 gated1 res1""".split()
        s = {n: ctx.enter_context(nc.semaphore(f"s_{n}")) for n in names}

        def await_unit(eng, name, u, back=0, per=1, k=1):
            if not u.static or u.index >= back:
                eng.wait_ge(s[name], per * (u.index - back) + k)

        def await_group(eng, name, u, back=0, per=1, k=1):
            if not u.static or u.group >= back:
                eng.wait_ge(s[name], per * (u.group - back) + k)

        def await_alone(eng, name, u, back=0, per=1, k=1):
            if not u.static or u.index >= back:
                eng.wait_ge(s[name], per * (u.index - back) + k)
                eng.nop(nofuse=True)

        def await_x(eng, u):
            eng.wait_ge(s["xin_" + "AB"[u.stream]], 16 * u.turn + 16)

        def c_(name, j):
            return col[:, COLS[name][0] + j:COLS[name][0] + j + 1]

        def row_all(name):
            return row[:, ROWS.index(name), :].unsqueeze(1).broadcast_to([P, T, H])

        def tokens(m, u):
            return m[:, :, bass.ds(u.group * GB, GB)].unsqueeze(3).broadcast_to([P, C, GB, S])

        def by_seq(ap):
            return ap.rearrange("p c (b s) -> p c b s", b=GB)

        def by_chunk(bk):
            return bk[:, :].rearrange("p (c n) -> p c n", c=2)

        def raw(ap):
            return ap.bitcast(F32)

        def split_parts(name):
            kind, l = name[:2], int(name[2])
            if kind == "qk":
                return [w[:, :, :].rearrange("p c n -> p (c n)") for w in wqk[l]]
            if kind == "vo":
                return [w[:, :, :].rearrange("p c n -> p (c n)") for w in wvo[l]]
            part_no = "ab".index(name[3])
            if kind == "w1":
                return [w[:, part_no].rearrange("p c n -> p (c n)") for w in w1[l]]
            half = HC // 2
            return [w[:, part_no * half:(part_no + 1) * half].rearrange("p c n -> p (c n)") for w in w2[l]]

        def place(n):
            return n if n < FIRST else (n - FIRST) % RING

        def await_piece(eng, name):
            n = PIECES.index(name)
            eng.wait_ge(s[f"piece_in{place(n)}"], 16 if n < FIRST else 16 * ((n - FIRST) // RING) + 32)

        def staged(name):
            at = place(PIECES.index(name))
            if at < RING:
                return ring[:, at, :]
            if at == RING:
                return hid[:, :, :, :].rearrange("p a e n -> p (a e n)")
            at -= RING + 1
            if at < 2:
                return prob[:, at].rearrange("p r h k -> p (r h k)")
            return probt[:, at - 2].rearrange("p r q n -> p (r q n)")

        def await_lo(eng, name):
            if name in SPLIT_POOL:
                eng.wait_ge(s["w_lo_pool"], SPLIT_POOL.index(name) + 1)
            else:
                eng.wait_ge(s["w_lo_dve"], SPLIT_DVE.index(name) + 1)

        def ada_bank(name):
            return {"ada1": b_mlp, "ada2": b_mix[0], "c0": b_mlp, "c1": b_turn, "c2": b_mlp}[name]

        def late_pieces(u):
            return SPLIT_LATE.get(u.index, []) if u.static else []

        def first_of_layer(u):
            return u.static and u.index == 2 * u.layer

        def chained(m):
            return m is not None and m.layer == 0

        def before(m):
            if m is None or (m.static and m.index == 0) or chained(Unit(m.r, m.c - 1)):
                return None
            return Unit(m.r, m.c - 1)

        def run_slots(eng, slot):
            slot(Unit(0, 0), None, Unit(0, 1))
            for q in range(1, 5):
                slot(Unit(0, q), Unit(0, q - 1), Unit(0, q + 1))
            with eng.Fori(1, ROUNDS) as i:
                for q in range(1, 5):
                    slot(Unit(i, q), Unit(i, q - 1), Unit(i, q + 1))
            for q in range(1, 4):
                slot(Unit(ROUNDS, q), Unit(ROUNDS, q - 1), Unit(ROUNDS, q + 1) if q < 3 else None)
            slot(None, Unit(ROUNDS, 3), None)

        block = ctx.enter_context(nc.Block())

        @block.sync
        def _(sp):
            def load_x(u):
                if not u.static or u.turn >= 1:
                    await_alone(sp, "xn0", u, back=4, per=T, k=T)
                    await_alone(sp, "base0", u, back=4)
                sp.dma_start(xin[u.stream][:, :, :], x_g[u.group]).then_inc(s["xin_" + "AB"[u.stream]], 16)

            def load_gate(w, u):
                await_group(sp, f"gated{w}", u, back=1)
                await_group(sp, f"gate_bias{w}", u, back=1)
                for half in range(2):
                    sp.dma_start(gate[w][64 * half:64 * half + 64, :, :],
                                 gates_g[u.group, w, half].partition_broadcast(64)).then_inc(s[f"gate_in{w}"], 16)

            def load_piece(n):
                if n >= FIRST:
                    old = PIECES[n - FIRST if n - FIRST < RING else n - RING]
                    if old in ADAPTIVE:
                        sp.wait_ge(s["ada_mm"], ADAPTIVE.index(old) + 1)
                    else:
                        sp.wait_ge(s["w_hi"], SPLIT.index(old) + 1)
                        await_lo(sp, old)
                sp.dma_start(staged(PIECES[n]), pieces[n]).then_inc(s[f"piece_in{place(n)}"], 16)

            def swap_values(u):
                await_unit(sp, "v_done", u)
                await_unit(sp, "vpairs_done", u, back=1, per=4, k=4)
                for half in range(2):
                    sp.dma_start(vswap[64 * half:64 * half + 64, :, :], vt[64 - 64 * half:128 - 64 * half, :, :])\
                      .then_inc(s["v_swapped"], 16)

            def store(u):
                await_alone(sp, "res1", u)
                sp.dma_start(out_g[u.group], xout[:, :, :]).then_inc(s["out_stored"], 16)

            def slot(a, m, nx):
                if a is not None and a.layer == 1:
                    load_gate(0, a)
                if a is not None:
                    swap_values(a)
                for name in {1: ("w11b", "w21a"), 2: ("w21b",)}.get(a.index, ()) if a is not None and a.static else ():
                    load_piece(PIECES.index(name))
                if before(m) is not None:
                    store(before(m))
                if m is not None and m.layer == 1:
                    load_gate(1, m)
                if a is None:
                    store(m)

            def round_(i):
                for q in range(1, 5):
                    if q in (2, 3):
                        load_x(Unit(i, q + 2))
                    slot(Unit(i, q), Unit(i, q - 1), Unit(i, q + 1))

            load_x(Unit(0, 0))
            load_piece(0)
            sp.dma_start(ident[:, :], ident_in).then_inc(s["const_in"], 16)
            sp.dma_start(cond[:, :, :], cond_t.rearrange("(c p) b -> p c b", p=P)).then_inc(s["const_in"], 16)
            sp.dma_start(col[:, :], cols).then_inc(s["const_in"], 16)
            for n in range(1, 4):
                load_piece(n)
            sp.dma_start(row[:, :, :], rows.partition_broadcast(P)).then_inc(s["rows_in"], 16)
            for half in range(2):
                sp.dma_start(mask8[64 * half:64 * half + 64, :, :],
                             mask.rearrange("(t h) k -> h t k", h=2)[half].partition_broadcast(64))\
                  .then_inc(s["rows_in"], 16)
            load_piece(4)
            load_x(Unit(0, 1))
            for n in range(5, FIRST + RING):
                load_piece(n)
            swap_values(Unit(0, 0))
            for n in range(FIRST + RING, FIRST + 2 * RING):
                load_piece(n)
            sp.wait_ge(s["ada_read"], ADA_READS)
            sp.dma_start(gates_dram.rearrange("w b f -> b w f"), gate_rows[:, :, :]).then_inc(s["gate_out"], 16)
            sp.wait_ge(s["gate_out"], 16)
            round_(0)
            with sp.Fori(1, ROUNDS) as i:
                round_(i)
            for q in range(1, 4):
                slot(Unit(ROUNDS, q), Unit(ROUNDS, q - 1), None)
            slot(None, Unit(ROUNDS, 3), None)
            sp.wait_ge(s["out_stored"], 16 * NG)

        @block.tensor
        def _(pe):
            def product(o, n_k, lhs, rhs, moving=False, lo_wait=None):
                for k in range(n_k):
                    for weight in range(2):
                        pair = (weight, 0) if moving else (0, weight)
                        pe.matmul(o, lhs(k, pair[0]), rhs(k, pair[1]), start=(k == 0 and weight == 0), stop=False)
                if lo_wait is not None:
                    lo_wait()
                for k in range(n_k):
                    mm = pe.matmul(o, lhs(k, 0 if moving else 1), rhs(k, 1 if moving else 0), start=False,
                                   stop=(k == n_k - 1))
                return mm

            def out_products_hi(bk, n_k, x_, w, cols_, hi_wait):
                first = True
                for ks in (range(n_k - 2), range(n_k - 2, n_k)):
                    for t in range(T):
                        for k in ks:
                            hi_wait(t, k)
                            for weight in range(2):
                                pe.matmul(bk[:, t * H:(t + 1) * H], x_[0][:, k, t * P:(t + 1) * P],
                                          w[weight][:, k, cols_], start=first, stop=False)
                                first = False

            def out_products_lo(bk, n_k, x_, w, cols_, ts=range(T)):
                for t in ts:
                    for k in range(n_k):
                        mm = pe.matmul(bk[:, t * H:(t + 1) * H], x_[1][:, k, t * P:(t + 1) * P], w[0][:, k, cols_],
                                       start=False, stop=(t == T - 1 and k == n_k - 1))
                return mm

            def turn(src, bk):
                for t in range(T):
                    for c in range(C):
                        mm = pe.transpose(bk[:, c * G + t * P:c * G + (t + 1) * P],
                                          src[:, t, c * P:(c + 1) * P], ident[:, :])
                return mm

            def turn_norm0(u):
                await_unit(pe, "xn0", u, per=T, k=T)
                turn(xn[0], b_turn).then_inc(s["turned0"], 1)

            def adaptive(name):
                await_piece(pe, name)
                if name == "c0":
                    pe.wait_ge(s["ada_read"], READS[0])
                elif name == "c1":
                    await_unit(pe, "mod0", Unit(0, 0))
                elif name == "c2":
                    pe.wait_ge(s["ada_read"], sum(READS[:3]))
                bk = ada_bank(name)
                cc = cond if name in ("ada1", "ada2") else silu_cond
                w = staged(name).rearrange("p (c n) -> p c n", c=C)
                if cc is silu_cond:
                    pe.wait_ge(s["silu"], 1)
                for j in FEATURE_CHUNKS[name]:
                    for k in range(C):
                        mm = pe.matmul(bk[:, j * B:(j + 1) * B], w[:, k, j * P:(j + 1) * P], cc[:, k, :],
                                       start=(k == 0), stop=(k == C - 1))
                if name in GATE_COLUMNS:
                    a = GATE_COLUMNS[name]
                    for k in range(C):
                        mm = pe.matmul(bk[0:B, 256:512], cc[:, k, :], w[:, k, a:a + H],
                                       start=(k == 0), stop=(k == C - 1))
                mm.then_inc(s["ada_mm"], 1)

            def project(u):
                w, x_ = wqk[u.layer], nrm[0]
                if first_of_layer(u):
                    await_lo(pe, f"qk{u.layer}")
                await_unit(pe, "hi0", u)
                for which, name in ((1, "k_mm"), (0, "q_mm")):
                    await_unit(pe, "pt_done", u, back=1, per=4, k=which + 1)
                    if name == "q_mm" and u.static and u.index == 0:
                        pe.wait_ge(s["ada_read"], sum(READS[:2]))
                    if name == "q_mm":
                        await_unit(pe, "y_lo", u, back=1, per=T, k=T)
                    for c in range(C):
                        a = which * H + c * P
                        mm = product(b_mix[which][:, c * G:(c + 1) * G], C, lambda k, h: w[h][:, k, a:a + P],
                                     lambda k, h: x_[h][:, k, :], moving=True,
                                     lo_wait=lambda: which == 1 and c == 0 and await_unit(pe, "lo0", u))
                    mm.then_inc(s[name], 1)
                if first_of_layer(u):
                    await_lo(pe, f"vo{u.layer}")
                await_unit(pe, "y_lo", u, back=1, per=T, k=T)
                for t in range(T):
                    mm = product(b_v[:, t * H:(t + 1) * H], C, lambda k, h: x_[h][:, k, t * P:(t + 1) * P],
                                 lambda k, h: wvo[u.layer][h][:, k, 0:H])
                mm.then_inc(s["v_mm"], 1)

            def scores(u, t, r):
                if t == 0 and r == 0:
                    await_alone(pe, "q_done", u, per=C, k=C)
                    await_alone(pe, "kheads_act", u)
                    await_alone(pe, "kheads_dve", u, per=HT - 1, k=HT - 1)
                if t == 1 and r == 1:
                    await_alone(pe, "v_done", u)
                rows_ = slice(64 * r, 64 * r + 64)
                for c in range(C):
                    for j in range(2):
                        b = slice((2 * t + j) * S, (2 * t + j + 1) * S)
                        mm = pe.matmul(b_score[t][r][64 * j:64 * j + 64, c * HT * S:(c + 1) * HT * S],
                                       qt[rows_, c, b], kheads[rows_, c, :, b], start=True, stop=True)
                mm.then_inc(s["score_mm"], 1)

            def turn_norm1(u):
                await_unit(pe, "xn1", u, per=T, k=T)
                turn(xn[1], b_turn).then_inc(s["turned1"], 1)

            def hidden(u, a):
                w = w1[u.layer]
                if first_of_layer(u):
                    await_lo(pe, f"w1{u.layer}a")
                    await_lo(pe, f"w1{u.layer}b")
                await_unit(pe, "hi1", u)
                for jp in range(HP):
                    if jp == 3:
                        await_unit(pe, "h_f32", u, per=HC, k=2)
                    elif jp == 2:
                        await_unit(pe, "mod1", u)
                    elif a is not None:
                        await_unit(pe, ("q_done", "k_done")[jp], a, per=C, k=C)
                    else:
                        await_unit(pe, "pt_done", u, per=4, k=jp + 1)
                    for e in range(2):
                        j = 2 * jp + e
                        hc = slice(j % 4 * P, j % 4 * P + P)
                        mm = product(b_hid[jp][:, e * G:(e + 1) * G],
                                     C, lambda k, h: w[h][:, j // 4, k, hc], lambda k, h: nrm[1][h][:, k, :],
                                     moving=True, lo_wait=lambda: j == 0 and await_unit(pe, "lo1", u))
                    mm.then_inc(s["w1_mm"], 1)

            def mlp_out_hi(u):
                await_unit(pe, "res1", u, back=1)
                if first_of_layer(u):
                    await_lo(pe, f"w2{u.layer}b")

                def hidden_hi(t, k):
                    if t == 0 and k % 2 == 0:
                        await_unit(pe, "h_hi", u, per=HP, k=k // 2 + 1)

                out_products_hi(b_mlp, HC, ht, w2[u.layer], slice(0, H), hidden_hi)

            def mlp_out_lo(u, ts=range(T)):
                await_unit(pe, "h_lo_pool", u, per=HP // 2, k=HP // 2)
                await_unit(pe, "h_lo_dve", u, per=HP // 2, k=HP // 2)
                mm = out_products_lo(b_mlp, HC, ht, w2[u.layer], slice(0, H), ts)
                if ts[-1] == T - 1:
                    mm.then_inc(s["w2_mm"], 1)

            def turn_probs(u, m, t):
                for r in range(RT):
                    await_unit(pe, "exp_done", u, per=4, k=r + 1 if t == 0 else 4)
                    if t == 0 and m is not None:
                        await_unit(pe, "h_f32", m, per=HC, k=(8, 4)[r])
                    elif t == 0:
                        await_unit(pe, ("q_done", "k_done")[r], u, per=C, k=C)
                    for q in range(4):
                        mm = pe.transpose(b_pt[t][r][:, q * P:(q + 1) * P],
                                          prob[:, t, r, 2 * q:2 * q + 2, :].rearrange("p h k -> p (h k)"), ident[:, :])
                    mm.then_inc(s["pt_mm"], 1)

            def values(u, t):
                for r in range(RT):
                    if t == 0 and r == 0:
                        await_alone(pe, "vpairs_done", u, per=4, k=4)
                    await_alone(pe, "pt_done", u, per=4, k=2 * t + r + 1)
                    for q in range(4):
                        pair = 4 * (q // 2) + 2 * r + q % 2
                        for j in range(2):
                            mm = pe.matmul(b_y[t][64 * j:64 * j + 64, pair * PAIR:(pair + 1) * PAIR],
                                           probt[:, t, r, q, 64 * j:64 * j + 64], vpairs[:, 2 * t + j, pair, :],
                                           start=True, stop=True)
                mm.then_inc(s["pv_mm"], 1)

            def turn_y(u, t):
                await_unit(pe, "y_done", u, per=T, k=t + 1)
                for c in range(C):
                    mm = pe.transpose(b_yt[t][:, c * P:(c + 1) * P], yn[:, t, c * P:(c + 1) * P], ident[:, :])
                mm.then_inc(s["y_turned"], 1)

            def attention_out(u):
                out_products_hi(b_wo, C, yt, wvo[u.layer], slice(H, 2 * H),
                                lambda t, k: k == 0 and await_unit(pe, "y_hi", u, per=T, k=t + 1))
                await_unit(pe, "y_lo", u, per=T, k=T)
                out_products_lo(b_wo, C, yt, wvo[u.layer], slice(H, 2 * H)).then_inc(s["wo_mm"], 1)

            pe.wait_ge(s["const_in"], 16 * CONSTS)
            adaptive("ada1")
            turn_norm0(Unit(0, 0))
            adaptive("ada2")

            def slot(a, m, nx):
                first = m is None
                if a is not None:
                    project(a)
                    scores(a, 0, 0)
                if m is not None:
                    turn_norm1(m)
                if a is not None:
                    scores(a, 0, 1)
                    scores(a, 1, 0)
                    scores(a, 1, 1)
                if m is not None:
                    hidden(m, a)
                    mlp_out_hi(m)
                    if chained(m) or a is None:
                        mlp_out_lo(m)
                if first:
                    adaptive("c0")
                    adaptive("c1")

                def turn_next():
                    if nx is not None:
                        if m is None:
                            pe.wait_ge(s["ada_read"], sum(READS[:4]))
                        else:
                            await_unit(pe, "h_f32", m, per=HC, k=6)
                        turn_norm0(nx)

                if a is not None:
                    late = m is not None and not chained(m)
                    if late:
                        mlp_out_lo(m, [0])
                    turn_probs(a, m, 0)
                    if first:
                        adaptive("c2")
                    turn_probs(a, m, 1)
                    values(a, 0)
                    if not chained(m):
                        turn_next()
                    values(a, 1)
                    if chained(m):
                        turn_next()
                    turn_y(a, 0)
                    if late:
                        mlp_out_lo(m, [1])
                    turn_y(a, 1)
                    attention_out(a)
                    if first:
                        pe.wait_ge(s["ada_read"], ADA_READS)

            run_slots(pe, slot)

        @block.scalar
        def _(act):
            def split_hi(name):
                await_piece(act, name)
                act.activation(split_parts(name)[0], staged(name), ACT.Copy).then_inc(s["w_hi"], 1)

            def norm_hi(w, u):
                await_unit(act, f"mod{w}", u)
                if w == 1:
                    await_unit(act, "w1_mm", u, back=1, per=HP, k=HP)
                else:
                    await_unit(act, "v_mm", u, back=1)
                act.activation(nrm[w][0][:, :, :], mod[w][:, :, :], ACT.Copy).then_inc(s[f"hi{w}"], 1)

            act.wait_ge(s["const_in"], 16 * CONSTS)
            act.activation(silu_cond[:, :, :], cond[:, :, :], ACT.Silu).then_inc(s["silu"], 1)
            for name in SPLIT[:2]:
                split_hi(name)
            norm_hi(0, Unit(0, 0))

            def slot(a, m, nx):
                if a is not None:
                    for name, dst in (("k", kt), ("q", qt)):
                        await_unit(act, f"{name}_mm", a)
                        if name == "q":
                            await_unit(act, "score_mm", a, back=1, per=4, k=4)
                        else:
                            await_unit(act, "kheads_dve", a, back=1, per=HT - 1, k=HT - 1)
                        for c in range(C):
                            act.activation(dst[:, c, :], b_mix["qk".index(name)][:, c * G:(c + 1) * G], ACT.Identity,
                                           bias=c_(f"b{name}{a.layer}", c)).then_inc(s[f"{name}_done"], 1)
                        if name == "k":
                            await_unit(act, "k_done", a, per=C, k=C)
                            await_unit(act, "score_mm", a, back=1, per=4, k=4)
                            act.activation(kheads[:, :, HT - 1, :], kt[:, :, :], ACT.Copy, scale=c_("head", HT - 1))\
                               .then_inc(s["kheads_act"], 1)
                    for name in late_pieces(a):
                        split_hi(name)
                if m is not None:
                    norm_hi(1, m)
                    await_unit(act, "w2_mm", m, back=1)
                    for jp in range(HP):
                        await_unit(act, "w1_mm", m, per=HP, k=jp + 1)
                        taken = ("h_lo_pool", "h_lo_dve")[jp % 2]
                        if jp >= 2:
                            await_unit(act, taken, m, per=HP // 2, k=1)
                        else:
                            await_unit(act, taken, m, back=1, per=HP // 2, k=HP // 2)
                        for e in range(2):
                            j = 2 * jp + e
                            act.activation(hid[:, jp % 2, e, :], b_hid[jp][:, e * G:(e + 1) * G], ACT.Gelu,
                                           bias=c_(f"b1{m.layer}", j)).then_inc(s["h_f32"], 1)
                        await_unit(act, "h_f32", m, per=HC, k=2 * jp + 2)
                        act.activation(ht[0][:, 2 * jp:2 * jp + 2, :], hid[:, jp % 2], ACT.Copy).then_inc(s["h_hi"], 1)
                else:
                    for name in ("w10a", "w10b", "w20a", "w20b"):
                        split_hi(name)
                if a is not None:
                    for t in range(T):
                        for r in range(RT):
                            await_unit(act, "shifted", a, per=4, k=2 * t + r + 1)
                            act.activation(prob[:, t, r], prob[:, t, r], ACT.Exp, scale=SCORE_SCALE[a.layer])\
                               .then_inc(s["exp_done"], 1)
                    for t in range(T):
                        for r in range(RT):
                            await_unit(act, "pt_mm", a, per=4, k=2 * t + r + 1)
                            await_unit(act, "pv_mm", a, back=1, per=T, k=T)
                            if t == 0 and r == 0 and m is None:
                                await_lo(act, "w20b")
                            act.activation(probt[:, t, r], b_pt[t][r][:, :].rearrange("p (q n) -> p q n", q=4), ACT.Copy)\
                               .then_inc(s["pt_done"], 1)
                    await_unit(act, "wo_mm", a, back=1)
                    for t in range(T):
                        await_unit(act, "y_turned", a, per=T, k=t + 1)
                        act.activation(yt[0][:, :, t * P:(t + 1) * P],
                                       b_yt[t][:, 0:H].rearrange("p (c n) -> p c n", c=C), ACT.Copy)\
                           .then_inc(s["y_hi"], 1)
                    if nx is not None:
                        norm_hi(0, nx)
                    await_unit(act, "gelu_table", a, back=1)
                    act.activation(table_probe[:, :], col[:, 0:1], ACT.Gelu).then_inc(s["gelu_table"], 1)

            run_slots(act, slot)

        @block.vector
        def _(dve):
            def split_lo(name):
                dve.wait_ge(s["w_hi"], SPLIT.index(name) + 1)
                hi, lo = split_parts(name)
                dve.tensor_tensor(lo, staged(name), raw(hi), ALU.subtract).then_inc(s["w_lo_dve"], 1)

            def adaptive(name):
                n = ADAPTIVE.index(name)
                dve.wait_ge(s["ada_mm"], n + 1)
                for j, (dst, chunk, plus) in FEATURE_TARGETS(name, scale, shift).items():
                    dve.tensor_scalar(dst[:, chunk, :], ada_bank(name)[:, j * B:(j + 1) * B], c_(name, j), plus,
                                      ALU.add, ALU.add).then_inc(s["ada_read"], 1)
                if name in GATE_COLUMNS:
                    w = 0 if name == "c1" else 1
                    dve.tensor_tensor(gate_rows[:, w, :], ada_bank(name)[0:B, 256:512], row[0:B, ROWS.index(f"bg{w}"), :],
                                      ALU.add).then_inc(s["ada_read"], 1)

            def stats_of(w, u, src):
                for t in range(T):
                    dve.bn_stats(stats[w][:, t, :], src[:, t, :]).then_inc(s[f"stat{w}"], 1)

            def variance_of(w, u):
                await_alone(dve, f"stat{w}", u, per=T, k=T)
                for t in range(T):
                    dve.bn_aggr(moments[w][:, t, :], stats[w][:, t, :]).then_inc(s[f"aggr{w}"], 1)
                await_unit(dve, f"aggr{w}", u, per=T, k=T)
                dve.tensor_scalar(var_eps[w][:, :], moments[w][:, :, 1], EPS, None, ALU.add).then_inc(s[f"var{w}"], 1)

            def normed(w, u, src):
                await_unit(dve, f"rstd{w}", u)
                await_unit(dve, f"turned{w}", u, back=1)
                for t in range(T):
                    dve.tensor_scalar(xn[w][:, t, :], src[:, t, :], moments[w][:, t, 0:1], rstd[w][:, t:t + 1],
                                      ALU.subtract, ALU.mult).then_inc(s[f"xn{w}"], 1)

            def source(u):
                return xin[u.stream] if u.layer == 0 else xres[u.stream]

            def times_scale(w, u):
                await_unit(dve, f"turned{w}", u)
                await_unit(dve, f"lo{w}", u, back=1)
                dve.tensor_tensor(by_seq(mod[w][:, :, :]), by_seq(by_chunk(b_turn)), tokens(scale[u.layer][w], u),
                                  ALU.mult).then_inc(s[f"scaled{w}"], 1)

            def plus_shift(w, u):
                await_unit(dve, f"scaled{w}", u)
                dve.tensor_tensor(by_seq(mod[w][:, :, :]), by_seq(mod[w][:, :, :]), tokens(shift[u.layer][w], u),
                                  ALU.add).then_inc(s[f"mod{w}"], 1)

            def modulate(w, u):
                times_scale(w, u)
                plus_shift(w, u)

            def norm_lo(w, u):
                await_unit(dve, f"hi{w}", u)
                dve.tensor_tensor(nrm[w][1][:, :, :], mod[w][:, :, :], raw(nrm[w][0][:, :, :]), ALU.subtract)\
                   .then_inc(s[f"lo{w}"], 1)

            def residual(w, u, bk):
                await_unit(dve, ("wo_mm", "w2_mm")[w], u)
                product = by_chunk(bk)
                if u.layer == 1:
                    dve.wait_ge(s[f"gate_in{w}"], 32 * u.group + 32)
                    if w == 1:
                        if not (u.static and u.group == 0):
                            dve.wait_ge(s["out_stored"], 16 * u.group)
                        dve.tensor_tensor(xout[:, :, :], product, gate[w][:, :, :], ALU.mult).then_inc(s["gated1"], 1)
                        return
                    await_unit(dve, "base0", u)
                    dve.tensor_tensor(xres[u.stream][:, :, :], product, gate[w][:, :, :], ALU.mult)\
                       .then_inc(s["gated0"], 1)
                    await_group(dve, "gated0", u)
                    product = xres[u.stream][:, :, :]
                else:
                    await_unit(dve, f"base{w}", u)
                dve.tensor_tensor(xres[u.stream][:, :, :], product, part[w][:, :, :], ALU.add)\
                   .then_inc(s[f"res{w}"], 1)

            def pair_values(u, swapped):
                if swapped:
                    await_unit(dve, "v_swapped", u, per=32, k=32)
                else:
                    await_unit(dve, "v_done", u)
                    await_unit(dve, "pv_mm", u, back=1, per=T, k=T)
                for odd in range(2):
                    half = slice(64 * odd, 64 * odd + 64)
                    src = (vt, vswap)[swapped][half, :, :].rearrange("p t (n o d) -> p t n o d", n=NPAIR, o=2)
                    dve.tensor_copy(vpairs[half, odd ^ swapped:GB:2, :, odd * (HD + 1):odd * (HD + 1) + HD],
                                    src[:, :, :, odd, :]).then_inc(s["vpairs_done"], 1)

            def softmax(u, t, rs=range(RT)):
                for r in rs:
                    k = 2 * t + r + 1
                    src = b_score[t][r][:, :].rearrange("p (h k) -> p h k", h=C * HT)
                    dst = prob[:, t, r]
                    await_unit(dve, "score_mm", u, per=4, k=k)
                    await_unit(dve, "pt_mm", u, back=1, per=4, k=4)
                    if k == 1 and u.static and u.index == 0:
                        await_lo(dve, "w10a")
                    if u.layer == 0:
                        dve.tensor_tensor(dst, src, maskf[:, t, :].unsqueeze(1).broadcast_to([P, C * HT, S]),
                                          ALU.add).then_inc(s["masked"], 1)
                        await_group(dve, "masked", u, per=4, k=k)
                        src = dst
                    dve.tensor_reduce(top[:, t, r, :], src, AX.X, ALU.max).then_inc(s["topped"], 1)
                    await_unit(dve, "topped", u, per=4, k=k)
                    dve.tensor_tensor(dst, src, top[:, t, r, :].unsqueeze(2).broadcast_to([P, C * HT, S]),
                                      ALU.subtract).then_inc(s["shifted"], 1)

            dve.memset(vpairs[:, :, :, :], 0.0).then_inc(s["dve_ready"], 1)
            dve.wait_ge(s["dve_ready"], 1)
            dve.memset(vpairs[0:64, :, :, HD:HD + 1], 1.0).then_inc(s["dve_ready"], 1)
            dve.memset(vpairs[64:128, :, :, PAIR - 1:PAIR], 1.0).then_inc(s["dve_ready"], 1)
            dve.wait_ge(s["dve_ready"], 3)
            await_x(dve, Unit(0, 0))
            stats_of(0, Unit(0, 0), xin[0])
            variance_of(0, Unit(0, 0))
            normed(0, Unit(0, 0), xin[0])
            dve.wait_ge(s["const_in"], 16 * CONSTS)
            adaptive("ada1")
            dve.wait_ge(s["ada_read"], READS[0])
            modulate(0, Unit(0, 0))
            split_lo("qk0")
            norm_lo(0, Unit(0, 0))
            adaptive("ada2")
            split_lo("vo0")
            dve.wait_ge(s["rows_in"], 16 * ROW_LOADS)

            def lo_of_hidden(jp, u):
                await_unit(dve, "h_hi", u, per=HP, k=jp + 1)
                if jp == 1:
                    await_unit(dve, "w2_mm", u, back=1)
                dve.tensor_tensor(ht[1][:, 2 * jp:2 * jp + 2, :], hid[:, jp % 2], raw(ht[0][:, 2 * jp:2 * jp + 2, :]),
                                  ALU.subtract).then_inc(s["h_lo_dve"], 1)

            def slot(a, m, nx):
                if a is not None:
                    await_unit(dve, "k_done", a, per=C, k=C)
                    await_unit(dve, "score_mm", a, back=1, per=4, k=4)
                    for j in range(HT - 1):
                        dve.tensor_scalar(kheads[:, :, j, :], kt[:, :, :], c_("head", j), None, ALU.mult)\
                           .then_inc(s["kheads_dve"], 1)
                if m is not None:
                    normed(1, m, xres[m.stream])
                if a is not None:
                    await_unit(dve, "v_mm", a)
                    await_unit(dve, "vpairs_done", a, back=1, per=4, k=4)
                    dve.tensor_tensor(vt[:, :, :], by_chunk(b_v), row_all(f"bv{a.layer}"), ALU.add)\
                       .then_inc(s["v_done"], 1)
                if before(m) is not None:
                    residual(1, before(m), b_mlp)
                if m is not None:
                    modulate(1, m)
                if a is not None:
                    pair_values(a, 0)
                    if a.layer == 0:
                        await_group(dve, "masked", a, back=1, per=4, k=4)
                        dve.tensor_scalar(maskf[:, :, :], mask8[:, bass.ds(a.group * T, T), :], -BIG, BIG,
                                          ALU.mult, ALU.mult).then_inc(s["mask_ready"], 1)
                        await_group(dve, "mask_ready", a)
                if m is not None:
                    norm_lo(1, m)
                if m is None:
                    split_lo("w10b")
                if a is not None:
                    softmax(a, 0)
                if m is not None:
                    lo_of_hidden(1, m)
                if a is not None:
                    softmax(a, 1, [0])
                if m is not None:
                    lo_of_hidden(3, m)
                if a is not None:
                    softmax(a, 1, [1])
                early = nx is not None and not chained(m)
                if early:
                    await_x(dve, nx)
                    stats_of(0, nx, source(nx))
                    variance_of(0, nx)
                if m is not None:
                    if a is not None:
                        pair_values(a, 1)
                    if chained(m) or a is None:
                        residual(1, m, b_mlp)
                else:
                    adaptive("c0")
                    adaptive("c1")
                    dve.wait_ge(s["ada_read"], sum(READS[:4]))
                    pair_values(a, 1)

                def take_y(t):
                    sums = b_y[t][:, 0:NPAIR * PAIR].rearrange("p (h n) -> p h n", h=NH)
                    await_unit(dve, "pv_mm", a, per=T, k=t + 1)
                    dve.reciprocal(inv[:, t, :], sums[:, :, HD]).then_inc(s["inv_done"], 1)
                    await_unit(dve, "inv_done", a, per=T, k=t + 1)
                    await_unit(dve, "y_turned", a, back=1, per=T, k=T)
                    dve.tensor_tensor(yn[:, t, :].rearrange("p (h d) -> p h d", h=NH), sums[:, :, 0:HD],
                                      inv[:, t, :].unsqueeze(2).broadcast_to([P, NH, HD]), ALU.mult)\
                       .then_inc(s["y_done"], 1)

                if a is None:
                    return
                if early:
                    normed(0, nx, source(nx))
                elif nx is not None:
                    await_unit(dve, "res1", m)
                    stats_of(0, nx, source(nx))
                    variance_of(0, nx)
                    normed(0, nx, source(nx))
                if m is None:
                    adaptive("c2")
                    dve.wait_ge(s["ada_read"], ADA_READS)
                take_y(0)
                if early:
                    times_scale(0, nx)
                take_y(1)
                if early:
                    plus_shift(0, nx)
                if nx is not None and not early:
                    modulate(0, nx)
                for t in range(T):
                    await_unit(dve, "y_hi", a, per=T, k=t + 1)
                    at = slice(t * P, (t + 1) * P)
                    dve.tensor_tensor(yt[1][:, :, at], b_yt[t][:, 0:H].rearrange("p (c n) -> p c n", c=C),
                                      raw(yt[0][:, :, at]), ALU.subtract).then_inc(s["y_lo"], 1)
                if nx is not None:
                    norm_lo(0, nx)
                residual(0, a, b_wo)
                await_unit(dve, "res0", a)
                stats_of(1, a, xres[a.stream])
                variance_of(1, a)

            run_slots(dve, slot)

        @block.gpsimd
        def _(pool):
            def inverse_root(w, u):
                await_unit(pool, f"var{w}", u)
                pool.tensor_tensor(rstd[w][:, :], var_eps[w][:, :], minus_half[:, :], ALU.pow).then_inc(s[f"rstd{w}"], 1)

            def base(w, u, src):
                await_unit(pool, f"res{w}", u, back=1)
                bias = row_all(ROW_OF[w] + str(u.layer))
                if u.layer == 1:
                    pool.wait_ge(s[f"gate_in{w}"], 32 * u.group + 32)
                    pool.tensor_tensor(part[w][:, :, :], gate[w][:, :, :], bias, ALU.mult).then_inc(s[f"gate_bias{w}"], 1)
                    await_group(pool, f"gate_bias{w}", u)
                    bias = part[w][:, :, :]
                pool.tensor_tensor(part[w][:, :, :], src[:, :, :], bias, ALU.add).then_inc(s[f"base{w}"], 1)

            def split_lo(name):
                pool.wait_ge(s["w_hi"], SPLIT.index(name) + 1)
                hi, lo = split_parts(name)
                pool.tensor_tensor(lo, staged(name), raw(hi), ALU.subtract).then_inc(s["w_lo_pool"], 1)

            def output(u):
                await_group(pool, "gated1", u)
                await_unit(pool, "base1", u)
                pool.tensor_tensor(xout[:, :, :], xout[:, :, :], part[1][:, :, :], ALU.add).then_inc(s["res1"], 1)

            pool.memset(minus_half[:, :], -0.5).then_inc(s["pool_ready"], 1)
            pool.wait_ge(s["pool_ready"], 1)
            inverse_root(0, Unit(0, 0))
            for name in ("w10a", "w20a", "w20b"):
                split_lo(name)
            pool.wait_ge(s["rows_in"], 16 * ROW_LOADS)

            def slot(a, m, nx):
                if m is not None:
                    inverse_root(1, m)
                if a is not None:
                    if a.layer == 0:
                        await_x(pool, a)
                    else:
                        await_unit(pool, "res1", a, back=2)
                    base(0, a, xin[a.stream] if a.layer == 0 else xres[a.stream])
                if before(m) is not None:
                    output(before(m))
                if m is not None:
                    if chained(m):
                        await_unit(pool, "res0", m)
                        base(1, m, xres[m.stream])
                    if a is not None:
                        for name in late_pieces(a)[:2]:
                            split_lo(name)
                    for jp in (0, 2):
                        await_unit(pool, "h_hi", m, per=HP, k=jp + 1)
                        if jp == 0:
                            await_unit(pool, "w2_mm", m, back=1)
                        pool.tensor_tensor(ht[1][:, 2 * jp:2 * jp + 2, :], hid[:, jp % 2], raw(ht[0][:, 2 * jp:2 * jp + 2, :]),
                                           ALU.subtract).then_inc(s["h_lo_pool"], 1)
                if a is not None:
                    for name in late_pieces(a)[2:]:
                        split_lo(name)
                if nx is not None:
                    inverse_root(0, nx)
                if m is not None and not chained(m):
                    await_unit(pool, "res0", m)
                    base(1, m, xres[m.stream])
                if a is None:
                    output(m)

            run_slots(pool, slot)


ROW_OF = ("bo", "b2")
FEATURE_CHUNKS = {"ada1": range(4), "ada2": range(4), "c0": range(4), "c1": (2, 3), "c2": (0, 1)}
GATE_COLUMNS = {"c1": 0, "c2": H}
READS = [len(FEATURE_CHUNKS[n]) + (n in GATE_COLUMNS) for n in ADAPTIVE]
ADA_READS = sum(READS)
CONSTS = 3
ROW_LOADS = 3


def FEATURE_TARGETS(name, scale, shift):
    one, none = (scale, 1.0), (shift, 0.0)
    parts = {"ada1": {0: (one, 0, 0), 2: (none, 0, 0)}, "ada2": {0: (one, 0, 1), 2: (none, 0, 1)},
             "c0": {0: (none, 1, 0), 2: (one, 1, 0)}, "c1": {2: (none, 1, 1)}, "c2": {0: (one, 1, 1)}}[name]
    return {j + c: (kind[0][l][w], c, kind[1]) for j, (kind, l, w) in parts.items() for c in range(C)}


def kernel(x, cond_1024, mask_BxS_bf0, **w):
    import concourse.bacc as bacc
    from concourse.bass_utils import run_bass_kernel_spmd as run

    w = {k: np.asarray(v) for k, v in w.items()}

    def wide(m):
        return m.reshape(C, P, 2 * H).transpose(1, 0, 2).reshape(P, PIECE)

    def tall(m):
        return m.reshape(HC // 2, P, H).transpose(1, 0, 2).reshape(P, PIECE)

    L0 = {n: w[f"L0_cond_{n}"].T for n in ("w_adaln1", "w_adaln2", "wq", "wk", "wv", "wo", "w1", "w2")}
    L1 = {n.lower(): w[f"L1_cond_{n}"] for n in ("Wc", "Wq", "Wk", "Wv", "Wo", "W1", "W2")}
    pieces = {"ada1": wide(L0["w_adaln1"]), "ada2": wide(L0["w_adaln2"])}
    for j in range(3):
        pieces[f"c{j}"] = wide(L1["wc"][:, j * 512:(j + 1) * 512])
    for l, m in enumerate((L0, L1)):
        pieces[f"qk{l}"] = wide(np.concatenate([m["wq"], m["wk"]], 1))
        pieces[f"vo{l}"] = wide(np.concatenate([m["wv"], m["wo"]], 1))
        for j, h in enumerate("ab"):
            pieces[f"w1{l}{h}"] = wide(m["w1"][:, j * 512:(j + 1) * 512])
            pieces[f"w2{l}{h}"] = tall(m["w2"][j * 512:(j + 1) * 512])
    pieces = np.stack([pieces[n] for n in PIECES])

    def by_column(v):
        return v.reshape(-1, P).T

    bc = w["L1_cond_bc"]
    head = (np.arange(P)[:, None] % 64 // HD == np.arange(HT)[None, :]).astype(np.float32)
    cols = {"bq0": w["L0_cond_bq"], "bk0": w["L0_cond_bk"], "bq1": w["L1_cond_bq"], "bk1": w["L1_cond_bk"],
            "b10": w["L0_cond_b1"], "b11": w["L1_cond_b1"], "ada1": w["L0_cond_b_adaln1"],
            "ada2": w["L0_cond_b_adaln2"], "c0": bc[0:512], "c1": bc[512:1024], "c2": bc[1024:1536]}
    cols = np.concatenate([by_column(cols[n]) if n != "head" else head for n in COLS], 1)
    rows = {"bv0": w["L0_cond_bv"], "bo0": w["L0_cond_bo"], "b20": w["L0_cond_b2"], "bv1": w["L1_cond_bv"],
            "bo1": w["L1_cond_bo"], "b21": w["L1_cond_b2"], "bg0": bc[512:768], "bg1": bc[1280:1536]}
    rows = np.stack([rows[n] for n in ROWS])
    arrays = {"x": np.asarray(x), "cond_t": np.asarray(cond_1024).T, "mask": np.asarray(mask_BxS_bf0),
              "pieces": pieces, "cols": cols, "rows": rows, "ident": np.eye(P, dtype=np.float32)}
    arrays = {f"in_{k}": np.ascontiguousarray(v) for k, v in arrays.items()}

    nc = bacc.Bacc("TRN2", target_bir_lowering=False, num_devices=1, dynamic_dma_scratch_size=1024)
    aps = [nc.dram_tensor(k, v.shape, mybir.dt.from_np(v.dtype), kind="ExternalInput").ap() for k, v in arrays.items()]
    out = nc.dram_tensor("out", (B, S, H), F32, kind="ExternalOutput").ap()
    build(nc, *aps, out)
    return run(nc, [arrays], core_ids=[0]).results[0]["out"]
```
